# Optimizing a Trainium2 kernel written in Bass

```python
import numpy as np
import jax
import jax.numpy as jnp

def _softmax(x, axis=-1):
    return jax.nn.softmax(x, axis=axis)

def _gelu(x):
    return jax.nn.gelu(x, approximate=True)

def _silu(x):
    return jax.nn.silu(x)

def _sigmoid(x):
    return jax.nn.sigmoid(x)

def _layernorm(x, axis=-1, eps=1e-05):
    m = jnp.mean(x, axis=axis, keepdims=True)
    v = jnp.var(x, axis=axis, keepdims=True)
    return (x - m) / jnp.sqrt(v + eps)

def _scatter_add(tgt, idx, src, axis=0):
    return tgt.at[idx].add(src)

def _segment_sum(src, seg, n):
    return jax.ops.segment_sum(src, seg, n)
kernel_name = 'mk_perceiver_d1_seqx_r4_88277a'

def setup_inputs(seed: int=0):
    np.random.seed(seed)
    _w = jnp.asarray

    def _rec_inputs():
        import jax
        import jax.numpy as jnp
        _rk = jax.random.key(seed)
        x = 7.22e-05 + 1 * jax.random.normal(jax.random.fold_in(_rk, 1), (1, 128, 256), jnp.float32)
        _lenS = 128 - jax.random.randint(jax.random.fold_in(_rk, 7), (1,), 0, max(1, 128 // 4) + 1, jnp.int32)
        _lenS2 = 12544 - jax.random.randint(jax.random.fold_in(_rk, 8), (1,), 0, max(1, 12544 // 4) + 1, jnp.int32)
        _ctx_1024P = jax.random.normal(jax.random.fold_in(_rk, 11), (1, 16, 256), jnp.float32)
        _ctx_1024c = jax.random.dirichlet(jax.random.fold_in(_rk, 511), 0.3 * jnp.ones((16,), jnp.float32), (1, 12544))
        _ctx_1024t = jnp.einsum('bsk,bkd->bsd', _ctx_1024c, _ctx_1024P)
        _ctx_1024t = _ctx_1024t * jax.lax.rsqrt(jnp.mean(jnp.square(_ctx_1024t)) + 1e-12) * 0.953939
        ctx_1024 = 4.13588e-05 + 0.999923 * (_ctx_1024t + 0.3 * jax.random.normal(jax.random.fold_in(_rk, 611), (1, 12544, 256), jnp.float32))
        _validS = jnp.arange(128)[None, :] < _lenS[:, None]
        _validS2 = jnp.arange(12544)[None, :] < _lenS2[:, None]
        _causal = jnp.tril(jnp.ones((128, 128), dtype=bool))
        mask_BxSxS2_bf0 = jnp.logical_not(jnp.ones((1, 128, 12544), dtype=bool))
        return (x, ctx_1024, mask_BxSxS2_bf0)
    x, ctx_1024, mask_BxSxS2_bf0 = _rec_inputs()

    def _L0_xattn_setup():
        import jax, jax.numpy as jnp
        import numpy as np
        N_HEAD = 16
        D_MODEL = 256
        D_HEAD = D_MODEL // N_HEAD
        NEG_FILL = -10000000.0
        key = jax.random.key(seed)
        ks = jax.random.split(key, 10)
        B, S = (4, 512)
        scale = 1.0 / np.sqrt(D_MODEL)
        inp = {'q': jax.random.normal(ks[0], (B, S, D_MODEL), jnp.float32), 'k': jax.random.normal(ks[1], (B, S, D_MODEL), jnp.float32), 'v': jax.random.normal(ks[2], (B, S, D_MODEL), jnp.float32), 'attention_mask': jnp.zeros((B, S, S), dtype=bool), 'Wq': jax.random.normal(ks[3], (D_MODEL, D_MODEL), jnp.float32) * scale, 'bq': jnp.zeros((D_MODEL,), jnp.float32), 'Wk': jax.random.normal(ks[4], (D_MODEL, D_MODEL), jnp.float32) * scale, 'bk': jnp.zeros((D_MODEL,), jnp.float32), 'Wv': jax.random.normal(ks[5], (D_MODEL, D_MODEL), jnp.float32) * scale, 'bv': jnp.zeros((D_MODEL,), jnp.float32)}
        return inp
    _L0_xattn_all = _L0_xattn_setup()
    _L0_xattn_in = {k: v for k, v in _L0_xattn_all.items() if k in ('Wq', 'bq', 'Wk', 'bk', 'Wv', 'bv')}
    del _L0_xattn_all

    def _L0_attn_setup():
        import math
        import jax, jax.numpy as jnp
        import numpy as np
        B, S, D, H = (2, 512, 256, 16)
        HD = D // H
        key = jax.random.key(seed)
        k1, k2, k3 = jax.random.split(key, 3)
        h = jax.random.normal(k1, (B, S, D), dtype=jnp.float32)
        Wqvk = jax.random.normal(k2, (D, 3 * D), dtype=jnp.float32) * (1.0 / math.sqrt(D))
        Wo = jax.random.normal(k3, (D, D), dtype=jnp.float32) * (1.0 / math.sqrt(D))
        return {'h': h, 'Wqvk': Wqvk, 'Wo': Wo}
    _L0_attn_all = _L0_attn_setup()
    _L0_attn_in = {k: v for k, v in _L0_attn_all.items() if k in ('Wqvk', 'Wo')}
    del _L0_attn_all

    def _L0_ffn_setup():
        import jax, jax.numpy as jnp
        import numpy as np
        BLOCK = 32
        W_BITS = 4
        ACT_BITS = 16

        def act_qdq(x):
            qmax = 2.0 ** (ACT_BITS - 1) - 1.0
            scale = jnp.maximum(jnp.max(jnp.abs(x)) / qmax, 1e-12)
            return jnp.clip(jnp.round(x / scale), -qmax - 1.0, qmax) * scale

        def fixed_qdq_u16(x):
            scale = 1.0 / 65536.0
            return jnp.clip(jnp.round(x / scale), 0.0, 65535.0) * scale

        def lpbq_dequant(w):
            O, I = w.shape
            qmax = 2.0 ** (W_BITS - 1) - 1.0
            wb = w.reshape(O, I // BLOCK, BLOCK)
            s = jnp.maximum(jnp.max(jnp.abs(wb), axis=-1, keepdims=True) / qmax, 1e-12)
            wq = jnp.clip(jnp.round(wb / s), -qmax - 1.0, qmax) * s
            return wq.reshape(O, I)
        key = jax.random.key(seed)
        k1, k2, k3, k4 = jax.random.split(key, 4)
        B, S, H, I = (2, 1024, 256, 768)
        x = jax.random.normal(k1, (B, S, H), jnp.float32)
        w_gate = jax.random.normal(k2, (I, H), jnp.float32) * 0.02
        w_up = jax.random.normal(k3, (I, H), jnp.float32) * 0.02
        w_down = jax.random.normal(k4, (H, I), jnp.float32) * 0.02
        return {'x': x, 'w_gate': w_gate, 'w_up': w_up, 'w_down': w_down}
    _L0_ffn_all = _L0_ffn_setup()
    _L0_ffn_in = {k: v for k, v in _L0_ffn_all.items() if k in ('w_gate', 'w_up', 'w_down')}
    del _L0_ffn_all
    return {'x': x, 'ctx_1024': ctx_1024, 'mask_BxSxS2_bf0': mask_BxSxS2_bf0, 'L0_xattn_Wq': _L0_xattn_in['Wq'], 'L0_xattn_bq': _L0_xattn_in['bq'], 'L0_xattn_Wk': _L0_xattn_in['Wk'], 'L0_xattn_bk': _L0_xattn_in['bk'], 'L0_xattn_Wv': _L0_xattn_in['Wv'], 'L0_xattn_bv': _L0_xattn_in['bv'], 'L0_attn_Wqvk': _L0_attn_in['Wqvk'], 'L0_attn_Wo': _L0_attn_in['Wo'], 'L0_ffn_w_gate': _L0_ffn_in['w_gate'], 'L0_ffn_w_up': _L0_ffn_in['w_up'], 'L0_ffn_w_down': _L0_ffn_in['w_down']}

def reference(x, ctx_1024, mask_BxSxS2_bf0, L0_xattn_Wq, L0_xattn_bq, L0_xattn_Wk, L0_xattn_bk, L0_xattn_Wv, L0_xattn_bv, L0_attn_Wqvk, L0_attn_Wo, L0_ffn_w_gate, L0_ffn_w_up, L0_ffn_w_down):
    import jax
    import jax.numpy as jnp

    def _L0_xattn_ref(q, k, v, attention_mask, Wq, bq, Wk, bk, Wv, bv):
        import jax, jax.numpy as jnp
        import numpy as np
        N_HEAD = 16
        D_MODEL = 256
        D_HEAD = D_MODEL // N_HEAD
        NEG_FILL = -10000000.0
        B, Sq, _ = q.shape
        Sk = k.shape[1]
        qh = (q @ Wq.T + bq).reshape(B, Sq, N_HEAD, D_HEAD)
        kh = (k @ Wk.T + bk).reshape(B, Sk, N_HEAD, D_HEAD)
        vh = (v @ Wv.T + bv).reshape(B, Sk, N_HEAD, D_HEAD)
        scores = jnp.einsum('bqhd,bkhd->bhqk', qh, kh) / np.sqrt(D_HEAD)
        scores = jnp.where(attention_mask[:, None, :, :], NEG_FILL, scores)
        probs = jax.nn.softmax(scores, axis=-1)
        out = jnp.einsum('bhqk,bkhd->bqhd', probs, vh)
        return out.reshape(B, Sq, N_HEAD * D_HEAD)

    def _L0_attn_ref(h, Wqvk, Wo):
        import math
        import jax, jax.numpy as jnp
        import numpy as np
        B, S, D, H = (2, 512, 256, 16)
        HD = D // H
        b, s, d = h.shape
        qvk = (h @ Wqvk).reshape(b, s, 3, H, HD)
        q, v, k = (qvk[:, :, 0], qvk[:, :, 1], qvk[:, :, 2])
        scores = jnp.einsum('bshi,bthi->bsth', q, k)
        mask = jnp.where(jnp.arange(s)[None, :] > jnp.arange(s)[:, None], jnp.float32(-jnp.inf), jnp.float32(0.0))
        scores = scores + mask[None, :, :, None]
        scores = scores / math.sqrt(d)
        weights = jax.nn.softmax(scores, axis=2)
        wv = jnp.einsum('bsth,bthi->bshi', weights, v).reshape(b, s, d)
        return wv @ Wo

    def _L0_ffn_ref(x, w_gate, w_up, w_down):
        import jax, jax.numpy as jnp
        import numpy as np
        BLOCK = 32
        W_BITS = 4
        ACT_BITS = 16

        def act_qdq(x):
            qmax = 2.0 ** (ACT_BITS - 1) - 1.0
            scale = jnp.maximum(jnp.max(jnp.abs(x)) / qmax, 1e-12)
            return jnp.clip(jnp.round(x / scale), -qmax - 1.0, qmax) * scale

        def fixed_qdq_u16(x):
            scale = 1.0 / 65536.0
            return jnp.clip(jnp.round(x / scale), 0.0, 65535.0) * scale

        def lpbq_dequant(w):
            O, I = w.shape
            qmax = 2.0 ** (W_BITS - 1) - 1.0
            wb = w.reshape(O, I // BLOCK, BLOCK)
            s = jnp.maximum(jnp.max(jnp.abs(wb), axis=-1, keepdims=True) / qmax, 1e-12)
            wq = jnp.clip(jnp.round(wb / s), -qmax - 1.0, qmax) * s
            return wq.reshape(O, I)
        x = act_qdq(x)
        up = act_qdq(x @ lpbq_dequant(w_up).T)
        gate = act_qdq(x @ lpbq_dequant(w_gate).T)
        sig = fixed_qdq_u16(jax.nn.sigmoid(gate))
        gate = act_qdq(gate * sig)
        o = act_qdq(gate * up)
        return o @ lpbq_dequant(w_down).T
    x = x + _L0_xattn_ref(_layernorm(x, axis=-1), ctx_1024, ctx_1024, mask_BxSxS2_bf0, L0_xattn_Wq, L0_xattn_bq, L0_xattn_Wk, L0_xattn_bk, L0_xattn_Wv, L0_xattn_bv)
    x = x + _L0_attn_ref(_layernorm(x, axis=-1), L0_attn_Wqvk, L0_attn_Wo)
    x = x + _L0_ffn_ref(_layernorm(x, axis=-1), L0_ffn_w_gate, L0_ffn_w_up, L0_ffn_w_down)
    return x

_drawn_inputs = setup_inputs


def setup_inputs(seed=0):
    import zlib

    import numpy as np

    out = dict(_drawn_inputs(seed))
    spreads = {'L0_xattn_bq': (0.0, 0.338), 'L0_xattn_bk': (0.0, 0.8), 'L0_xattn_bv': (0.0, 0.1)}
    factors = {}
    for name, (base, spread) in spreads.items():
        noise = np.random.default_rng([zlib.crc32(name.encode()), seed]).standard_normal(out[name].shape)
        drawn = base * np.exp(spread * noise) if base else spread * noise
        out[name] = jnp.asarray(drawn.astype(out[name].dtype))
    for name, factor in factors.items():
        out[name] = (out[name] * factor).astype(out[name].dtype)
    return out
```

```python
import concourse.bass as bass
from concourse import mybir
from contextlib import ExitStack

H = 16
HD = 16
D = H * HD
Q = 128
SK = 12544
F = 768
P = 128
DC = D // P
KT = SK // P
T = 7
NB = KT // T
BK = T * P
HK = BK // 2
HT = H // DC
PR = H // 2
SLOTS = 3
SR = SLOTS * 2 * HD
VW = HD + 1
UNITS = 2 * T
MAGIC = 12582912.0
BIG = -float(2 ** 60)
BLOCK = 32
FT = F // P
FH = F // 2


def perceiver_layer(nc: bass.Bass, x_d, ctx_d, maskn_d, maskt_d, wqn_d, wqr_d, bqn_d, bqr_d, wk_d, bk_d, wv_d, bv_d,
                    wqvk_d, wo_d, wgate_d, wup_d, wdown_d, eye_d, headmask_d, pairmask_d, causal_d, out_d):
    f32, f32r, bf16 = mybir.dt.float32, mybir.dt.float32r, mybir.dt.bfloat16
    i32, u8 = mybir.dt.int32, mybir.dt.uint8
    ALU, ACT, AX = mybir.AluOpType, mybir.ActivationFunctionType, mybir.AxisListType

    k_hi_d = nc.dram_tensor("k_hi_scratch", [NB, DC, P, BK], f32, kind="Internal").ap()
    k_lo_d = nc.dram_tensor("k_lo_scratch", [NB, DC, P, BK], f32, kind="Internal").ap()
    v_d = nc.dram_tensor("v_scratch", [NB, P, T * H * VW], f32, kind="Internal").ap()

    with ExitStack() as stack_of_contexts:
        enter = stack_of_contexts.enter_context

        def sb(name, shape, dt=f32):
            return enter(nc.sbuf_tensor(name, shape, dt))

        def sem(name):
            return enter(nc.semaphore(name))

        early = sb("early", [P, 2 * DC * BK + 2 * BK + 2 * T * H * VW])
        ctx_t = early[:, 0:2 * DC * BK].rearrange("p (b c k) -> p b c k", b=2, c=DC)
        o1 = 2 * DC * BK
        kf = early[:, o1:o1 + 2 * BK].rearrange("p (m k) -> p m k", m=2)
        o2 = o1 + 2 * BK
        v_new = early[:, o2:o2 + 2 * T * H * VW].rearrange("p (b t h w) -> p b t h w", b=2, t=T, h=H)
        WN = 3 * DC * F
        w_raw = early[:, 0:WN]
        late = early[:, WN:WN + 4096]
        k_hi = sb("k_hi", [P, 2, DC, BK], f32r)
        k_lo = sb("k_lo", [P, DC, BK], f32r)
        k_stack = sb("k_stack", [P, 2, PR, BK], f32r)
        middle = sb("middle", [P, 4 * 8 * Q])
        mask_all = middle[:, 0:SK // 4].bitcast(i32)
        probs = middle[:, :].rearrange("p (s n) -> p s n", s=4)
        v_in = sb("v_in", [P, 2 * T * H * VW])
        v_ring = v_in[:, :].rearrange("p (b t h w) -> p b t h w", b=2, t=T, h=H)
        q_pad = sb("q_pad", [P, H, Q], f32r)
        q_stack = sb("q_stack", [P, PR, 2, Q], f32r)
        wqr = sb("wqr", [P, DC * PR * SR])
        wqn = sb("wqn", [P, DC, D])
        wk = sb("wk", [P, DC, D])
        wv = sb("wv", [P, DC, D])
        wqvk = sb("wqvk", [P, DC, 3 * D])
        wo = sb("wo", [P, DC, D])
        bqn = sb("bqn", [P, DC])
        bqr = sb("bqr", [P, PR])
        bk = sb("bk", [P, DC])
        bv = sb("bv", [P, D])
        eye = sb("eye", [P, P])
        head_mask = sb("head_mask", [P, HT])
        pair_mask = sb("pair_mask", [P, 2])
        causal = sb("causal", [P, P])
        causal_b = sb("causal_b", [P, P], bf16)
        big_eye = sb("big_eye", [P, P], bf16)
        zeros_b = sb("zeros_b", [P, 512], bf16)
        ones_c = sb("ones_c", [P, 1])
        mask_w = sb("mask_w", [P, 2, BK // 4], i32)
        mask_u = mask_w[:, :, :].rearrange("p b k -> p (b k)").bitcast(u8).rearrange("p (b k) -> p b k", b=2)
        mask_b = sb("mask_b", [P, 2, BK], bf16)
        x0 = sb("x0", [P, D])
        x1 = sb("x1", [P, D])
        x2 = sb("x2", [P, D])
        x3 = sb("x3", [P, D])
        xn = sb("xn", [P, D])
        xt = sb("xt", [P, DC, Q])
        block_max = sb("block_max", [P, 2, H])
        row_max = sb("row_max", [P, H])
        stats = sb("stats", [P, 24])
        small = sb("small", [P, 16])
        flag_f = sb("flag_f", [P, 1])
        flag_i = sb("flag_i", [1, 1], i32)
        w_scale = sb("w_scale", [P, WN // BLOCK])
        w_rec = sb("w_rec", [P, WN // BLOCK])

        ps_a = enter(nc.psum_tensor("ps_a", [P, 4, 512], f32))
        ps_k = enter(nc.psum_tensor("ps_k", [P, 2, 512], f32))
        ps_v = enter(nc.psum_tensor("ps_v", [P, 2, 512], f32))
        attended = ps_k[:, 0, :]

        x_in, eye_in, wqn_in, wqr_in, bq_in, masks_in = (sem(n) for n in ("x_in", "eye_in", "wqn_in", "wqr_in", "bq_in", "masks_in"))
        wk_in, wv_in, bk_in, bv_in, mask_all_in, attn_w_in, ffn_w_in = (
            sem(n) for n in ("wk_in", "wv_in", "bk_in", "bv_in", "mask_all_in", "attn_w_in", "ffn_w_in"))
        ctx_in = [sem(f"ctx_in{i}") for i in range(2)]
        mask_in = [sem(f"mask_in{i}") for i in range(2)]
        mask_t_in = [sem(f"mask_t_in{i}") for i in range(2)]
        hi_stored = [[sem(f"hi_stored{i}{m}") for m in range(DC)] for i in range(2)]
        lo_stored = [sem(f"lo_stored{m}") for m in range(DC)]
        v_stored = [sem(f"v_stored{i}") for i in range(2)]
        stack_in = [sem(f"stack_in{i}") for i in range(2)]
        v_back = [sem(f"v_back{i}") for i in range(2)]
        out_stored = sem("out_stored")
        consts_set = sem("consts_set")
        k_projected, k_evacuated, v_projected, v_evacuated = (
            sem(n) for n in ("k_projected", "k_evacuated", "v_projected", "v_evacuated"))
        hi_ready, lo_ready, mask_cast = sem("hi_ready"), sem("lo_ready"), sem("mask_cast")
        max_scored, max_taken = sem("max_scored"), sem("max_taken")
        row_max_ready, max_rows_ready, max_rows_set = sem("row_max_ready"), sem("max_rows_ready"), sem("max_rows_set")
        scored, exp_done, prob_slots_free, sums_done = (
            sem(n) for n in ("scored", "exp_done", "prob_slots_free", "sums_done"))
        sqrt_asked, sqrt_done = sem("sqrt_asked"), sem("sqrt_done")
        q_ready, q_projected, q_spread = sem("q_ready"), sem("q_projected"), sem("q_spread")
        normed, transposed, transposed_copied = sem("normed"), sem("transposed"), sem("transposed_copied")
        flag_asked, flag_summed, flag_ready = sem("flag_asked"), sem("flag_summed"), sem("flag_ready")
        sums_copied, sums_turned = sem("sums_copied"), sem("sums_turned")
        weights_ready, weights_turned, weights_copied = sem("weights_ready"), sem("weights_turned"), sem("weights_copied")
        qk_projected, v2_projected, qk_copied, v2_copied = (
            sem(n) for n in ("qk_projected", "v2_projected", "qk_copied", "v2_copied"))
        self_scored, self_shifted, self_exp, probs_turned, probs_copied, self_attended = (
            sem(n) for n in ("self_scored", "self_shifted", "self_exp", "probs_turned", "probs_copied", "self_attended"))
        wv_ready, wv_turned, wv_copied, wo_done = sem("wv_ready"), sem("wv_turned"), sem("wv_copied"), sem("wo_done")
        peak_ready, peak_spread = sem("peak_ready"), sem("peak_spread")
        ffn_projected, gate_ready, sig_ready = sem("ffn_projected"), sem("gate_ready"), sem("sig_ready")
        o_ready, o_turned, o_copied, down_done, result_ready = (
            sem(n) for n in ("o_ready", "o_turned", "o_copied", "down_done", "result_ready"))
        dve_steps, act_steps = sem("dve_steps"), sem("act_steps")

        s_probs = middle[:, 0:H * Q].rearrange("p (h k) -> p h k", h=H)
        s_probs_t = middle[:, H * Q:2 * H * Q].rearrange("p (h q) -> p h q", h=H)
        w_blocks = w_raw.rearrange("p (n b) -> p n b", b=BLOCK)
        up_raw = w_raw[:, 0:DC * F].rearrange("p (t i) -> p t i", t=FT)
        gate_raw = w_raw[:, DC * F:2 * DC * F].rearrange("p (t i) -> p t i", t=FT)
        down_raw = w_raw[:, 2 * DC * F:].rearrange("p (t i) -> p t i", t=DC)
        ffn_wt = v_in[:, 0:2 * DC * F].rearrange("p (w c o) -> p w c o", w=2, c=DC)
        down_wt = wqr[:, 0:FT * D].rearrange("p (t o) -> p t o", t=FT)
        q2_pad = late[:, 0:H * Q].rearrange("p (h q) -> p h q", h=H)
        k2_t = late[:, H * Q:H * Q + DC * Q].rearrange("p (m k) -> p m k", m=DC)
        v2_sb = late[:, 2304:2304 + H * VW].rearrange("p (h w) -> p h w", h=H)
        sums_sb = late[:, 2688:3200]
        both = late[:, 0:2 * F].rearrange("p (w f) -> p w f", w=2)
        up_q, gate_q = both[:, 0, :], both[:, 1, :]
        sig = late[:, 2 * F:3 * F]
        hidden = late[:, 3 * F:4 * F]
        hidden_t = middle[:, 0:F].rearrange("p (t q) -> p t q", t=FT)

        block = enter(nc.Block())

        @block.sync
        def _(sp):
            sp.dma_start(x0[:], x_d).then_inc(x_in, 16)
            sp.dma_start(wk[:], wk_d).then_inc(wk_in, 16)
            sp.dma_start(ctx_t[:, 0], ctx_d[0]).then_inc(ctx_in[0], 16)
            sp.dma_start(bk[:], bk_d).then_inc(bk_in, 16)
            sp.dma_start(wv[:], wv_d).then_inc(wv_in, 16)
            sp.dma_start(eye[:], eye_d).then_inc(eye_in, 16)
            sp.dma_start(wqn[:], wqn_d).then_inc(wqn_in, 16)
            sp.dma_start(wqr[:, :], wqr_d).then_inc(wqr_in, 16)
            sp.dma_start(bqn[:], bqn_d).then_inc(bq_in, 16)
            sp.dma_start(bqr[0:SR, :], bqr_d).then_inc(bq_in, 16)
            sp.dma_start(head_mask[:], headmask_d).then_inc(masks_in, 16)
            sp.dma_start(pair_mask[0:SR, :], pairmask_d).then_inc(masks_in, 16)
            sp.dma_start(causal[:], causal_d).then_inc(masks_in, 16)
            sp.dma_start(mask_w[:, 0, :], maskn_d[0]).then_inc(mask_in[0], 16)
            for b in range(NB):
                sp.dma_start(mask_all[:, b * BK // 4:(b + 1) * BK // 4], maskn_d[b]).then_inc(mask_all_in, 16)
            sp.dma_start(bv[:], bv_d).then_inc(bv_in, 16)
            sp.dma_start(wqvk[:], wqvk_d).then_inc(attn_w_in, 16)
            sp.dma_start(wo[:], wo_d).then_inc(attn_w_in, 16)

            def held(value):
                return value if isinstance(value, int) else sp.snap(value)

            def load(s, par):
                values, casts = held((s - 1) * T), held(s - 1)
                sp.wait_ge(v_projected, values)
                sp.wait_ge(mask_cast, casts)
                sp.dma_start(ctx_t[:, par], ctx_d[s]).then_inc(ctx_in[par], 16)
                sp.dma_start(mask_w[:, par, :], maskn_d[s]).then_inc(mask_in[par], 16)

            def store(s, par):
                for m in range(DC):
                    sp.wait_ge(hi_ready, s * DC + m + 1)
                    sp.dma_start(k_hi_d[s, m], k_hi[:, par, m, :].bitcast(f32)).then_inc(hi_stored[par][m], 16)
                    sp.wait_ge(lo_ready, s * DC + m + 1)
                    sp.dma_start(k_lo_d[s, m], k_lo[:, m, :].bitcast(f32)).then_inc(lo_stored[m], 16)
                sp.wait_ge(v_evacuated, s * T + T)
                sp.dma_start(v_d[s], v_new[:, par].rearrange("p t h w -> p (t h w)")).then_inc(v_stored[par], 16)

            with sp.Fori(0, (NB - 2) // 2) as i:
                load(i * 2 + 1, 1)
                store(i * 2, 0)
                load(i * 2 + 2, 0)
                store(i * 2 + 1, 1)
            load(NB - 1, 1)
            store(NB - 2, 0)
            store(NB - 1, 1)

            def load_back(b, par):
                for m in range(DC):
                    for slot in range(SLOTS):
                        src = (k_lo_d if slot == 2 else k_hi_d)[b, m]
                        sp.dma_start(k_stack[slot * 32:slot * 32 + 32, par, m * PR // 2:(m + 1) * PR // 2, :].bitcast(f32),
                                     src.rearrange("(p r) k -> r p k", r=2 * HD)).then_inc(stack_in[par], 16)
                sp.dma_start(v_in[:, par * T * H * VW:(par + 1) * T * H * VW], v_d[b]).then_inc(v_back[par], 16)

            for m in range(DC):
                for par in range(2):
                    sp.wait_ge(hi_stored[par][m], 16 * NB // 2)
                sp.wait_ge(lo_stored[m], 16 * NB)
            for par in range(2):
                sp.wait_ge(v_stored[par], 16 * NB // 2)
            for b in range(2):
                load_back(b, b)
            sp.wait_ge(v_projected, NB * T)
            sp.wait_ge(lo_ready, NB * DC)
            sp.dma_start(up_raw, wup_d).then_inc(ffn_w_in, 16)
            sp.dma_start(gate_raw, wgate_d).then_inc(ffn_w_in, 16)
            sp.dma_start(down_raw, wdown_d).then_inc(ffn_w_in, 16)
            with sp.Fori(1, NB // 2) as i:
                for par in range(2):
                    b = i * 2 + par
                    sp.wait_ge(prob_slots_free, (b - 1) * UNITS + 4)
                    load_back(b, par)
            sp.wait_ge(out_stored, 16)

        @block.gpsimd
        def _(pool):
            fills = (early[:, o2:],
                     k_stack[SR:SR + 1, :, :, :].bitcast(f32),
                     ones_c[:])
            for n, fill in enumerate(fills):
                nc.gpsimd.memset(fill, 1.0).then_inc(consts_set, 1)
                pool.wait_ge(consts_set, n + 1)
            nc.gpsimd.memset(zeros_b[:], 0.0).then_inc(consts_set, 1)
            pool.wait_ge(consts_set, 4)

            def split(s, par, first):
                if not first:
                    pool.wait_ge(max_scored, (s - 1) * H)
                for m in range(DC):
                    if not (first and par == 0 and m == 0):
                        pool.wait_ge(lo_ready, s * DC + m)
                    pool.wait_ge(k_evacuated, s * DC + m + 1)
                    if not first:
                        pool.wait_ge(hi_stored[par][m], (s - par) * 8)
                    nc.gpsimd.tensor_tensor(k_hi[:, par, m, :], kf[:, m, :], ones_c[:, 0:1].to_broadcast([P, BK]),
                                            ALU.mult).then_inc(hi_ready, 1)
                    pool.wait_ge(hi_ready, s * DC + m + 1)
                    if not (first and par == 0):
                        pool.wait_ge(lo_stored[m], s * 16)
                    nc.gpsimd.tensor_tensor(k_lo[:, m, :], kf[:, m, :], k_hi[:, par, m, :].bitcast(f32),
                                            ALU.subtract).then_inc(lo_ready, 1)

            split(0, 0, True)
            split(1, 1, True)
            with pool.Fori(1, NB // 2) as i:
                split(i * 2, 0, False)
                split(i * 2 + 1, 1, False)
            pool.wait_ge(mask_cast, NB)
            for b in range(2):
                pool.dma_start(mask_w[:, b, :], maskt_d[b]).then_inc(mask_t_in[b], 16)
            with pool.Fori(1, NB // 2) as i:
                for par in range(2):
                    pool.wait_ge(mask_cast, i * 2 + par + NB - 1)
                    pool.dma_start(mask_w[:, par, :], maskt_d[i * 2 + par]).then_inc(mask_t_in[par], 16)

        @block.scalar
        def _(act):
            steps = [0]

            def link(instruction):
                steps[0] += 1
                instruction.then_inc(act_steps, 1)
                act.wait_ge(act_steps, steps[0])

            act.wait_ge(sqrt_asked, 1)
            nc.scalar.activation(small[:, 1:2], small[:, 0:1], ACT.Sqrt).then_inc(sqrt_done, 1)
            act.wait_ge(bk_in, 16)
            act.wait_ge(consts_set, 1)

            def evacuate_keys(s, m, first):
                act.wait_ge(k_projected, s * DC + m + 1)
                if not first:
                    act.wait_ge(lo_ready, (s - 1) * DC + m + 1)
                nc.scalar.activation(kf[:, m, :].rearrange("p (n k) -> p n k", n=2), ps_k[:, :, 0:HK], ACT.Identity,
                                     bias=bk[:, m:m + 1]).then_inc(k_evacuated, 1)

            def evacuate_values(s, par, t):
                act.wait_ge(v_projected, s * T + t + 1)
                nc.scalar.copy(v_new[:, par, t, :, 0:HD],
                               ps_v[:, (par + t) % 2, 0:D].rearrange("p (h d) -> p h d", h=H)).then_inc(v_evacuated, 1)

            def evacuate(s, par, first):
                act.wait_ge(mask_in[par], (s - par) * 8 + 16)
                if not first:
                    act.wait_ge(max_scored, (s - 1) * H)
                nc.scalar.copy(mask_b[:, par, :], mask_u[:, par, :]).then_inc(mask_cast, 1)
                if not first:
                    act.wait_ge(v_stored[par], (s - par) * 8)
                evacuate_values(s, par, 0)
                evacuate_keys(s, 0, first and par == 0)
                for t in (1, 2, 3):
                    evacuate_values(s, par, t)
                evacuate_keys(s, 1, first and par == 0)
                for t in (4, 5, 6):
                    evacuate_values(s, par, t)

            evacuate(0, 0, True)
            evacuate(1, 1, True)
            with act.Fori(1, NB // 2) as i:
                evacuate(i * 2, 0, False)
                evacuate(i * 2 + 1, 1, False)

            act.wait_ge(max_rows_ready, 1)
            nc.scalar.mul(q_stack[SR:SR + 1, 0:PR // 2, :, :].rearrange("p a b q -> p (a b q)"),
                          ps_a[SR:SR + 1, 0:2, :].rearrange("p a q -> p (a q)"), -1.0).then_inc(max_rows_set, 1)

            with act.Fori(0, NB * UNITS // 4) as i:
                for u in range(4):
                    n = i * 4 + u
                    act.wait_ge(scored, n + 1)
                    act.wait_ge(prob_slots_free, n + 1)
                    half = u % 2
                    nc.scalar.activation(probs[:, u, :], ps_a[:, 2 * half:2 * half + 2, :].rearrange("p a n -> p (a n)"),
                                         ACT.Exp).then_inc(exp_done, 1)

            def copy_weights(n, dst):
                act.wait_ge(weights_turned, n + 1)
                nc.scalar.copy(dst, ps_v[:, n % 2, :]).then_inc(weights_copied, 1)

            flat_wt = v_in[:, 0:2 * DC * F]
            for n in range(6):
                copy_weights(n, flat_wt[:, n * 512:(n + 1) * 512])
            for n in range(3):
                copy_weights(6 + n, wqr[:, n * 512:(n + 1) * 512])

            act.wait_ge(sqrt_asked, 2)
            nc.scalar.activation(small[:, 1:2], small[:, 0:1], ACT.Sqrt).then_inc(sqrt_done, 1)
            for g in range(4):
                act.wait_ge(self_shifted, g + 1)
                nc.scalar.activation(s_probs[:, 4 * g:4 * g + 4, :], s_probs[:, 4 * g:4 * g + 4, :], ACT.Exp,
                                     scale=1.0 / D ** 0.5).then_inc(self_exp, 1)
            for g in range(4):
                act.wait_ge(probs_turned, g + 1)
                nc.scalar.copy(s_probs_t[:, 4 * g:4 * g + 4, :].rearrange("p h q -> p (h q)"),
                               ps_v[:, g % 2, :]).then_inc(probs_copied, 1)
            act.wait_ge(sqrt_asked, 3)
            nc.scalar.activation(small[:, 1:2], small[:, 0:1], ACT.Sqrt).then_inc(sqrt_done, 1)
            act.wait_ge(gate_ready, 1)
            nc.scalar.activation(sig, gate_q, ACT.Sigmoid).then_inc(sig_ready, 1)
            act.wait_ge(result_ready, 1)
            act.dma_start(out_d, x3[:]).then_inc(out_stored, 16)

        @block.vector
        def _(dve):
            steps = [0]

            def link(instruction):
                steps[0] += 1
                instruction.then_inc(dve_steps, 1)
                dve.wait_ge(dve_steps, steps[0])

            def layernorm(src, nth):
                link(nc.vector.bn_stats(stats[:, 0:6], src))
                link(nc.vector.bn_aggr(stats[:, 8:10], stats[:, 0:6]))
                nc.vector.tensor_scalar(small[:, 0:1], stats[:, 9:10], 1e-5, None, ALU.add).then_inc(sqrt_asked, 1)
                dve.wait_ge(sqrt_done, nth)
                link(nc.vector.reciprocal(small[:, 3:4], small[:, 1:2]))
                link(nc.vector.tensor_tensor(small[:, 4:5], small[:, 0:1], small[:, 3:4], ALU.mult))
                link(nc.vector.tensor_scalar(small[:, 5:6], small[:, 4:5], small[:, 1:2], 0.5, ALU.add, ALU.mult))
                link(nc.vector.reciprocal(small[:, 6:7], small[:, 5:6]))
                return nc.vector.tensor_scalar(xn[:], src, stats[:, 8:9], small[:, 6:7], ALU.subtract, ALU.mult)

            def copy_turned(nth, psum):
                dve.wait_ge(transposed, nth)
                nc.vector.tensor_copy(xt[:, :, :].rearrange("p c q -> p (c q)"), psum).then_inc(transposed_copied, 1)

            dve.wait_ge(x_in, 16)
            layernorm(x0[:], 1).then_inc(normed, 1)
            copy_turned(1, ps_a[:, 0, 0:D])
            dve.wait_ge(eye_in, 16)
            nc.vector.tensor_scalar(big_eye[:], eye[:], BIG, None, ALU.mult)
            dve.wait_ge(bq_in, 32)
            dve.wait_ge(masks_in, 48)
            nc.vector.tensor_copy(causal_b[:], causal[:])
            dve.wait_ge(q_projected, 1)
            for m in range(DC):
                link(nc.vector.tensor_scalar(x3[:, m * Q:(m + 1) * Q], ps_a[:, 1, m * Q:(m + 1) * Q], bqn[:, m:m + 1],
                                             HD ** -0.5, ALU.add, ALU.mult))
            for m in range(DC):
                last = nc.vector.tensor_tensor(
                    q_pad[:, m * HT:(m + 1) * HT, :],
                    x3[:, m * Q:(m + 1) * Q].unsqueeze(1).to_broadcast([P, HT, Q]),
                    head_mask[:, :].unsqueeze(2).to_broadcast([P, HT, Q]), ALU.mult)
            last.then_inc(q_ready, 1)
            qr = v_in[0:SR, 0:PR * Q].rearrange("p (a q) -> p a q", a=PR)
            qh = v_in[0:SR, PR * Q:2 * PR * Q].rearrange("p (a q) -> p a q", a=PR)
            dve.wait_ge(q_projected, 2)
            link(nc.vector.tensor_tensor(qr, ps_a[0:SR, 2:4, :].rearrange("p a (b q) -> p (a b) q", q=Q),
                                         bqr[0:SR, :].unsqueeze(2).to_broadcast([SR, PR, Q]), ALU.add))
            link(nc.vector.tensor_scalar(qr, qr, HD ** -0.5, None, ALU.mult))
            for ab in range(2):
                link(nc.vector.tensor_scalar(q_stack[0:SR, :, ab, :], qr, pair_mask[0:SR, ab:ab + 1], None, ALU.mult))
            for ab in range(2):
                lo = slice(32, 64)
                link(nc.vector.tensor_scalar(qh[lo], qr[lo], pair_mask[lo, ab:ab + 1], None, ALU.mult))
                link(nc.vector.tensor_tensor(q_stack[lo, :, ab, :], qh[lo], q_stack[lo, :, ab, :].bitcast(f32),
                                             ALU.subtract))
            nc.vector.memset(row_max[:], -3.0e38).then_inc(q_spread, 1)
            dve.wait_ge(mask_all_in, 16 * NB)
            nc.vector.tensor_reduce(flag_f[:], mask_all, AX.X, ALU.max).then_inc(flag_asked, 1)
            dve.wait_ge(flag_summed, 1)
            nc.vector.tensor_scalar(flag_i[0:1, 0:1], ps_v[0:1, 1, 0:1], 0.0, None, ALU.is_gt).then_inc(flag_ready, 1)

            def maxima(s, par):
                for h in range(H):
                    dve.wait_ge(max_scored, s * H + h + 1)
                    half = h % 2
                    nc.vector.tensor_reduce(block_max[:, par, h:h + 1], ps_a[:, 2 * half:2 * half + 2, 0:HK],
                                            AX.XY, ALU.max).then_inc(max_taken, 1)
                dve.wait_ge(max_taken, s * H + H)
                nc.vector.tensor_tensor(row_max[:], row_max[:], block_max[:, par, :], ALU.max).then_inc(row_max_ready, 1)
                dve.wait_ge(row_max_ready, s + 1)

            with dve.Fori(0, NB // 2) as i:
                maxima(i * 2, 0)
                maxima(i * 2 + 1, 1)

            dve.wait_ge(max_rows_ready, 2)
            nc.vector.tensor_scalar(q_stack[SR:SR + 1, PR // 2:PR, :, :].rearrange("p a b q -> p (a b q)"),
                                    ps_a[SR:SR + 1, 2:4, :].rearrange("p a q -> p (a q)"), -1.0, None,
                                    ALU.mult).then_inc(max_rows_set, 1)

            def cast_mask(par, nth_load, used):
                dve.wait_ge(mask_t_in[par], nth_load)
                dve.wait_ge(scored, used)
                nc.vector.tensor_copy(mask_b[:, par, :], mask_u[:, par, :]).then_inc(mask_cast, 1)

            for b in range(2):
                cast_mask(b, 16, 0)

            dve.wait_ge(ffn_w_in, 48)
            scale_b = w_scale[:, :].unsqueeze(2).to_broadcast([P, WN // BLOCK, BLOCK])
            rec_b = w_rec[:, :].unsqueeze(2).to_broadcast([P, WN // BLOCK, BLOCK])
            link(nc.vector.tensor_reduce(w_scale[:], w_blocks, AX.X, ALU.max, apply_absolute_value=True))
            link(nc.vector.tensor_scalar(w_scale[:], w_scale[:], 1.0 / 7.0, 1e-12, ALU.mult, ALU.max))
            link(nc.vector.reciprocal(w_rec[:], w_scale[:]))
            link(nc.vector.tensor_tensor(w_blocks, w_blocks, rec_b, ALU.mult))
            link(nc.vector.tensor_scalar(w_raw, w_raw, MAGIC, MAGIC, ALU.add, ALU.subtract))
            link(nc.vector.tensor_scalar(w_raw, w_raw, 7.0, -8.0, ALU.min, ALU.max))
            nc.vector.tensor_tensor(w_blocks, w_blocks, scale_b, ALU.mult).then_inc(weights_ready, 1)
            dve.wait_ge(bv_in, 16)
            link(nc.vector.tensor_tensor(x1[:], x0[:], bv[:], ALU.add))

            with dve.Fori(1, NB // 2) as i:
                for par in range(2):
                    cast_mask(par, i * 16 + 16, (i * 2 + par - 1) * UNITS)

            dve.wait_ge(sums_done, 1)
            nc.vector.tensor_copy(sums_sb, attended).then_inc(sums_copied, 1)
            dve.wait_ge(sums_turned, 1)
            turned = ps_k[:, 1, :].rearrange("p (h r) -> p h r", r=32)
            link(nc.vector.reciprocal(stats[:, 0:H], turned[:, :, HD]))
            link(nc.vector.tensor_tensor(xn[:, :].rearrange("p (h d) -> p h d", h=H), turned[:, :, 0:HD],
                                         stats[:, 0:H].unsqueeze(2).to_broadcast([P, H, HD]), ALU.mult))
            link(nc.vector.tensor_tensor(x1[:], x1[:], xn[:], ALU.add))

            layernorm(x1[:], 2).then_inc(normed, 1)
            copy_turned(2, ps_k[:, 0, 0:D])
            dve.wait_ge(qk_projected, 1)
            nc.vector.tensor_copy(x3[:], ps_k[:, 1, 0:D])
            link(nc.vector.tensor_copy(k2_t.rearrange("p m k -> p (m k)"), ps_k[:, 1, D:2 * D]))
            for m in range(DC):
                last = nc.vector.tensor_tensor(
                    q2_pad[:, m * HT:(m + 1) * HT, :],
                    x3[:, m * Q:(m + 1) * Q].unsqueeze(1).to_broadcast([P, HT, Q]),
                    head_mask[:, :].unsqueeze(2).to_broadcast([P, HT, Q]), ALU.mult)
            last.then_inc(qk_copied, 1)
            dve.wait_ge(v2_projected, 1)
            nc.vector.memset(v2_sb[:, :, HD:VW], 1.0)
            nc.vector.tensor_copy(v2_sb[:, :, 0:HD], ps_k[:, 0, D:2 * D].rearrange("p (h d) -> p h d", h=H)).then_inc(v2_copied, 1)
            for g in range(4):
                dve.wait_ge(self_scored, g + 1)
                scores = ps_a[:, g, :].rearrange("p (h k) -> p h k", h=4)
                link(nc.vector.tensor_reduce(block_max[:, 0, 4 * g:4 * g + 4], scores, AX.X, ALU.max))
                nc.vector.tensor_tensor(s_probs[:, 4 * g:4 * g + 4, :], scores,
                                        block_max[:, 0, 4 * g:4 * g + 4].unsqueeze(2).to_broadcast([P, 4, Q]),
                                        ALU.subtract).then_inc(self_shifted, 1)
            dve.wait_ge(self_attended, 1)
            summed = ps_k[:, 1, 0:H * VW].rearrange("p (h w) -> p h w", h=H)
            link(nc.vector.reciprocal(stats[:, 0:H], summed[:, :, HD]))
            nc.vector.tensor_tensor(xn[:, :].rearrange("p (h d) -> p h d", h=H), summed[:, :, 0:HD],
                                    stats[:, 0:H].unsqueeze(2).to_broadcast([P, H, HD]), ALU.mult).then_inc(wv_ready, 1)
            dve.wait_ge(wv_turned, 1)
            nc.vector.tensor_copy(xt[:, :, :].rearrange("p c q -> p (c q)"), ps_k[:, 0, 0:D]).then_inc(wv_copied, 1)
            dve.wait_ge(wo_done, 1)
            link(nc.vector.tensor_tensor(x2[:], ps_k[:, 1, 0:D], x1[:], ALU.add))

            def peaks(views, nth):
                for n, view in enumerate(views):
                    last = nc.vector.tensor_reduce(block_max[:, 1, n:n + 1], view,
                                                   AX.XY if len(view.shape) == 3 else AX.X, ALU.max, apply_absolute_value=True)
                last.then_inc(peak_ready, 1)
                dve.wait_ge(peak_spread, nth)
                link(nc.vector.tensor_reduce(small[:, 8:8 + len(views)],
                                             ps_k[:, 1, 0:len(views) * P].rearrange("p (n k) -> p n k", k=P), AX.X, ALU.max))
                link(nc.vector.tensor_scalar(small[:, 8:8 + len(views)], small[:, 8:8 + len(views)], 1.0 / 32767.0, 1e-12,
                                             ALU.mult, ALU.max))
                link(nc.vector.reciprocal(small[:, 10:10 + len(views)], small[:, 8:8 + len(views)]))

            def quantise(dst, src, n):
                link(nc.vector.tensor_scalar(dst, src, small[:, 10 + n:11 + n], MAGIC, ALU.mult, ALU.add))
                link(nc.vector.tensor_scalar(dst, dst, MAGIC, 32767.0, ALU.subtract, ALU.min))
                return nc.vector.tensor_scalar(dst, dst, -32768.0, small[:, 8 + n:9 + n], ALU.max, ALU.mult)

            link(layernorm(x2[:], 3))
            peaks([xn[:]], 1)
            quantise(xn[:], xn[:], 0).then_inc(normed, 1)
            copy_turned(3, ps_k[:, 0, 0:D])
            dve.wait_ge(ffn_projected, 1)
            up_ps, gate_ps = ps_a[:, 0:2, 0:FH], ps_a[:, 2:4, 0:FH]
            peaks([up_ps, gate_ps], 2)
            quantise(gate_q.rearrange("p (n f) -> p n f", n=2), gate_ps, 1).then_inc(gate_ready, 1)
            link(quantise(up_q.rearrange("p (n f) -> p n f", n=2), up_ps, 0))
            dve.wait_ge(sig_ready, 1)
            link(nc.vector.tensor_scalar(sig, sig, 65536.0, MAGIC, ALU.mult, ALU.add))
            link(nc.vector.tensor_scalar(sig, sig, MAGIC, 0.0, ALU.subtract, ALU.max))
            link(nc.vector.tensor_scalar(sig, sig, 65535.0, 1.0 / 65536.0, ALU.min, ALU.mult))
            link(nc.vector.tensor_tensor(hidden, gate_q, sig, ALU.mult))
            peaks([hidden], 3)
            link(quantise(hidden, hidden, 0))
            link(nc.vector.tensor_tensor(hidden, hidden, up_q, ALU.mult))
            peaks([hidden], 4)
            quantise(hidden, hidden, 0).then_inc(o_ready, 1)
            for n in range(2):
                dve.wait_ge(o_turned, n + 1)
                nc.vector.tensor_copy(hidden_t[:, 3 * n:3 * n + 3, :].rearrange("p t q -> p (t q)"),
                                      ps_v[:, n, 0:3 * Q]).then_inc(o_copied, 1)
            dve.wait_ge(down_done, 1)
            nc.vector.tensor_tensor(x3[:], ps_k[:, 0, 0:D], x2[:], ALU.add).then_inc(result_ready, 1)

        @block.tensor
        def _(pe):
            def project_keys(s, par, m, n):
                if n == 0 and not (isinstance(s, int) and s == 0 and m == 0):
                    pe.wait_ge(k_evacuated, s * DC + m)
                for c in range(DC):
                    last = nc.tensor.matmul(ps_k[:, n, 0:HK], wk[:, c, m * P:(m + 1) * P],
                                            ctx_t[:, par, c, n * HK:(n + 1) * HK], start=(c == 0), stop=(c == DC - 1))
                if n == 1:
                    last.then_inc(k_projected, 1)

            def project_values(s, par, t):
                if not (isinstance(s, int) and s == 0 and t < 2):
                    pe.wait_ge(v_evacuated, s * T + t - 1)
                for c in range(DC):
                    last = nc.tensor.matmul(ps_v[:, (par + t) % 2, 0:D], ctx_t[:, par, c, t * P:(t + 1) * P],
                                            wv[:, c, :], start=(c == 0), stop=(c == DC - 1))
                last.then_inc(v_projected, 1)

            projections = [("k", 0, 0), ("v", 0), ("k", 0, 1), ("v", 1), ("v", 2), None, ("k", 1, 0), ("v", 3), None,
                           ("k", 1, 1), ("v", 4), None, ("v", 5), None, ("v", 6), None]

            def project(s, par, slot):
                work = projections[slot]
                if work is None:
                    return
                if work[0] == "k":
                    project_keys(s, par, *work[1:])
                else:
                    project_values(s, par, work[1])

            def score_for_max(s, par, h, masked):
                m = h // HT
                if h % HT == 0:
                    pe.wait_ge(hi_ready, s * DC + m + 1)
                if h == 0 and masked:
                    pe.wait_ge(mask_cast, s + 1)
                if not (isinstance(s, int) and s == 0 and h < 2):
                    pe.wait_ge(max_taken, s * H + h - 1)
                for n in range(2):
                    out = ps_a[:, 2 * (h % 2) + n, 0:HK]
                    last = nc.tensor.matmul(out, q_pad[:, h, :], k_hi[:, par, m, n * HK:(n + 1) * HK],
                                            start=True, stop=not masked)
                    if masked:
                        last = nc.tensor.matmul(out, big_eye[:], mask_b[:, par, n * HK:(n + 1) * HK], start=False, stop=True)
                last.then_inc(max_scored, 1)

            pe.wait_ge(wk_in, 16)
            pe.wait_ge(ctx_in[0], 16)
            pe.wait_ge(wv_in, 16)
            for slot in range(H):
                project(0, 0, slot)
            pe.wait_ge(normed, 1)
            pe.wait_ge(eye_in, 16)
            for c in range(DC):
                last = nc.tensor.transpose(ps_a[:, 0, c * Q:(c + 1) * Q], xn[:, c * P:(c + 1) * P], eye[:])
            last.then_inc(transposed, 1)
            pe.wait_ge(transposed_copied, 1)
            pe.wait_ge(wqn_in, 16)
            for m in range(DC):
                for c in range(DC):
                    last = nc.tensor.matmul(ps_a[:, 1, m * Q:(m + 1) * Q], wqn[:, c, m * P:(m + 1) * P], xt[:, c, :],
                                            start=(c == 0), stop=(c == DC - 1))
            last.then_inc(q_projected, 1)
            pe.wait_ge(wqr_in, 16)
            wqr_v = wqr[:, :].rearrange("p (c a r) -> p c a r", c=DC, a=PR)
            for a in range(PR):
                for c in range(DC):
                    last = nc.tensor.matmul(ps_a[0:SR, 2 + a // 4, (a % 4) * Q:(a % 4 + 1) * Q], wqr_v[:, c, a, :], xt[:, c, :],
                                            start=(c == 0), stop=(c == DC - 1))
            last.then_inc(q_projected, 1)
            pe.wait_ge(flag_asked, 1)
            pe.wait_ge(consts_set, 4)
            pe.wait_ge(v_evacuated, T)
            nc.tensor.matmul(ps_v[0:1, 1, 0:1], flag_f[:], ones_c[:], start=True, stop=True).then_inc(flag_summed, 1)
            pe.wait_ge(flag_ready, 1)
            masked_flag = pe.value_load(flag_i[0:1, 0:1], min_val=0, max_val=1)

            def attend(masked):
                pe.wait_ge(q_ready, 1)
                pe.wait_ge(q_spread, 1)

                def step(s, par):
                    pe.wait_ge(ctx_in[par], (s - par) * 8 + 16)
                    for slot in range(H):
                        project(s, par, slot)
                        score_for_max(s - 1, 1 - par, slot, masked)

                step(1, 1)
                with pe.Fori(1, NB // 2) as i:
                    step(i * 2, 0)
                    step(i * 2 + 1, 1)
                for h in range(H):
                    score_for_max(NB - 1, 1, h, masked)

                pe.wait_ge(row_max_ready, NB)
                for h in range(H):
                    last = nc.tensor.matmul(ps_a[SR:SR + 1, h // 4, (h % 4) * Q:(h % 4 + 1) * Q], row_max[:, h:h + 1], eye[:],
                                            start=True, stop=True)
                    if h % HT == HT - 1:
                        last.then_inc(max_rows_ready, 1)

                pe.wait_ge(k_evacuated, NB * DC)
                nc.tensor.matmul(attended, zeros_b[:, 0:P], zeros_b[:], start=True, stop=True,
                                 skip_group_check=True).then_inc(prob_slots_free, 4)
                pe.wait_ge(max_rows_set, 2)

                def score(n, b_par, t, half):
                    for a in range(4):
                        bank = 2 * half + a // 2
                        last = nc.tensor.matmul(ps_a[:, bank, (a % 2) * 2 * Q:(a % 2 + 1) * 2 * Q],
                                                k_stack[0:SR + 1, b_par, 4 * half + a, t * P:(t + 1) * P],
                                                q_stack[0:SR + 1, 4 * half + a, :, :].rearrange("p b q -> p (b q)"),
                                                start=(a % 2 == 0), stop=(a % 2 == 1) and not masked, skip_group_check=True)
                        if masked and a % 2 == 1:
                            last = nc.tensor.matmul(ps_a[:, bank, :], big_eye[:],
                                                    mask_b[:, b_par, t * P:(t + 1) * P].unsqueeze(1).to_broadcast([P, 4, Q]),
                                                    start=False, stop=True, skip_group_check=True)
                    last.then_inc(scored, 1)

                def add_up(n, b_par, t, half, slot):
                    pe.wait_ge(exp_done, n + 1)
                    for k in range(8):
                        h = 8 * half + k
                        j, c = h % 4, h // 4
                        last = nc.tensor.matmul(attended[32 * j:32 * j + VW, c * Q:(c + 1) * Q], v_ring[:, b_par, t, h, :],
                                                probs[:, slot, k * Q:(k + 1) * Q], start=False, stop=False,
                                                skip_group_check=True)
                    last.then_inc(prob_slots_free, 1)

                def arrive(b, par):
                    pe.wait_ge(stack_in[par], (b - par) * 48 + 96)
                    if masked:
                        pe.wait_ge(mask_cast, b + NB + 1)

                def two_blocks(i, final):
                    for u in range(2 * UNITS):
                        n = i * (2 * UNITS) + u
                        if not (final and u == 2 * UNITS - 1):
                            nxt = (u + 1) % (2 * UNITS)
                            if nxt == 0:
                                arrive(i * 2 + 2, 0)
                            if nxt == UNITS:
                                arrive(i * 2 + 1, 1)
                            score(None, nxt // UNITS, nxt % UNITS // 2, nxt % 2)
                        if u % UNITS == 0:
                            pe.wait_ge(v_back[u // UNITS], i * 16 + 16)
                        add_up(n, u // UNITS, u % UNITS // 2, u % 2, u % 4)

                arrive(0, 0)
                score(None, 0, 0, 0)
                with pe.Fori(0, NB // 2 - 1) as i:
                    two_blocks(i, False)
                two_blocks(NB // 2 - 1, True)

            for masked in (False, True):
                with pe.If(masked_flag == int(masked)):
                    attend(masked)

            nc.tensor.matmul(ps_v[0:1, 0, 0:1], zeros_b[:, 0:1], zeros_b[:, 0:1], start=True, stop=True).then_inc(sums_done, 1)
            pe.wait_ge(sums_copied, 1)
            for c in range(4):
                last = nc.tensor.transpose(ps_k[:, 1, c * P:(c + 1) * P], sums_sb[:, c * P:(c + 1) * P], eye[:])
            last.then_inc(sums_turned, 1)

            pe.wait_ge(weights_ready, 1)
            tiles = [(raw, t, c) for raw in (up_raw, gate_raw) for c in range(DC) for t in range(FT)]
            tiles += [(down_raw, o, t) for t in range(FT) for o in range(DC)]
            for n, (raw, t, c) in enumerate(tiles):
                group = n // 4
                if n % 4 == 0 and group >= 2:
                    pe.wait_ge(weights_copied, group - 1)
                last = nc.tensor.transpose(ps_v[:, group % 2, (n % 4) * P:(n % 4 + 1) * P], raw[:, t, c * P:(c + 1) * P], eye[:])
                if n % 4 == 3:
                    last.then_inc(weights_turned, 1)

            def turn_rows(nth):
                pe.wait_ge(normed, nth)
                for c in range(DC):
                    last = nc.tensor.transpose(ps_k[:, 0, c * Q:(c + 1) * Q], xn[:, c * P:(c + 1) * P], eye[:])
                last.then_inc(transposed, 1)
                pe.wait_ge(transposed_copied, nth)

            turn_rows(2)
            pe.wait_ge(attn_w_in, 32)
            for n, at in enumerate((0, P, 2 * D, 2 * D + P)):
                for c in range(DC):
                    last = nc.tensor.matmul(ps_k[:, 1, n * Q:(n + 1) * Q], wqvk[:, c, at:at + P], xt[:, c, :],
                                            start=(c == 0), stop=(c == DC - 1))
            last.then_inc(qk_projected, 1)
            for c in range(DC):
                last = nc.tensor.matmul(ps_k[:, 0, D:2 * D], xt[:, c, :], wqvk[:, c, D:2 * D], start=(c == 0), stop=(c == DC - 1))
            last.then_inc(v2_projected, 1)
            pe.wait_ge(qk_copied, 1)
            for g in range(4):
                for k in range(4):
                    h = 4 * g + k
                    nc.tensor.matmul(ps_a[:, g, k * Q:(k + 1) * Q], q2_pad[:, h, :], k2_t[:, h // HT, :], start=(k == 0),
                                     stop=False, skip_group_check=True)
                nc.tensor.matmul(ps_a[:, g, :], big_eye[:], causal_b[:, :].unsqueeze(1).to_broadcast([P, 4, Q]),
                                 start=False, stop=True, skip_group_check=True).then_inc(self_scored, 1)
            pe.wait_ge(weights_copied, 9)
            pe.wait_ge(v2_copied, 1)

            def attend_self(g):
                pe.wait_ge(probs_copied, g + 1)
                for k in range(4):
                    h = 4 * g + k
                    last = nc.tensor.matmul(ps_k[:, 1, h * VW:(h + 1) * VW], s_probs_t[:, h, :], v2_sb[:, h, :],
                                            start=True, stop=True, skip_group_check=True)
                return last

            for g in range(4):
                pe.wait_ge(self_exp, g + 1)
                if g >= 2:
                    attend_self(g - 2)
                for k in range(4):
                    last = nc.tensor.transpose(ps_v[:, g % 2, k * P:(k + 1) * P], s_probs[:, 4 * g + k, :], eye[:])
                last.then_inc(probs_turned, 1)
            attend_self(2)
            attend_self(3).then_inc(self_attended, 1)
            pe.wait_ge(wv_ready, 1)
            for c in range(DC):
                last = nc.tensor.transpose(ps_k[:, 0, c * Q:(c + 1) * Q], xn[:, c * P:(c + 1) * P], eye[:])
            last.then_inc(wv_turned, 1)
            pe.wait_ge(wv_copied, 1)
            for c in range(DC):
                last = nc.tensor.matmul(ps_k[:, 1, 0:D], xt[:, c, :], wo[:, c, :], start=(c == 0), stop=(c == DC - 1))
            last.then_inc(wo_done, 1)

            def spread_peaks(nth, count):
                pe.wait_ge(peak_ready, nth)
                for n in range(count):
                    last = nc.tensor.matmul(ps_k[:, 1, n * P:(n + 1) * P], block_max[:, 1, n:n + 1].to_broadcast([P, P]), eye[:],
                                            start=True, stop=True)
                last.then_inc(peak_spread, 1)

            spread_peaks(1, 1)
            turn_rows(3)
            for w in range(2):
                for n in range(2):
                    for c in range(DC):
                        last = nc.tensor.matmul(ps_a[:, 2 * w + n, 0:FH], xt[:, c, :], ffn_wt[:, w, c, n * FH:(n + 1) * FH],
                                                start=(c == 0), stop=(c == DC - 1))
            last.then_inc(ffn_projected, 1)
            spread_peaks(2, 2)
            spread_peaks(3, 1)
            spread_peaks(4, 1)
            pe.wait_ge(o_ready, 1)
            for t in range(FT):
                last = nc.tensor.transpose(ps_v[:, t // 3, (t % 3) * Q:(t % 3 + 1) * Q], hidden[:, t * P:(t + 1) * P], eye[:])
                if t % 3 == 2:
                    last.then_inc(o_turned, 1)
            for t in range(FT):
                if t % 3 == 0:
                    pe.wait_ge(o_copied, t // 3 + 1)
                last = nc.tensor.matmul(ps_k[:, 0, 0:D], hidden_t[:, t, :], down_wt[:, t, :], start=(t == 0), stop=(t == FT - 1))
            last.then_inc(down_done, 1)


def kernel(x, ctx_1024, mask_BxSxS2_bf0, L0_xattn_Wq, L0_xattn_bq, L0_xattn_Wk, L0_xattn_bk, L0_xattn_Wv, L0_xattn_bv,
           L0_attn_Wqvk, L0_attn_Wo, L0_ffn_w_gate, L0_ffn_w_up, L0_ffn_w_down):
    import numpy as np
    import concourse.bacc as bacc
    from concourse.bass_utils import run_bass_kernel_spmd

    def chunks(w):
        return np.ascontiguousarray(np.asarray(w).reshape(-1, P, np.asarray(w).shape[1]).transpose(1, 0, 2))

    def words(a):
        return np.ascontiguousarray(a).view(np.int32)

    mask = np.asarray(mask_BxSxS2_bf0)[0].view(np.uint8)
    wq_t = chunks(np.asarray(L0_xattn_Wq).T)
    rows = np.arange(P)
    arrays = {
        "x": np.asarray(x)[0],
        "ctx": np.asarray(ctx_1024)[0].T.reshape(DC, P, NB, BK).transpose(2, 1, 0, 3),
        "maskn": words(mask.reshape(Q, NB, BK).transpose(1, 0, 2)),
        "maskt": words(mask.T.reshape(NB, T, P, Q).transpose(0, 2, 1, 3).reshape(NB, P, T * Q)),
        "wqn": wq_t,
        "wqr": np.broadcast_to(wq_t.reshape(P, DC, PR, 1, 2 * HD), (P, DC, PR, SLOTS, 2 * HD)).reshape(P, DC * PR * SR),
        "bqn": np.asarray(L0_xattn_bq).reshape(DC, P).T,
        "bqr": np.broadcast_to(np.asarray(L0_xattn_bq).reshape(1, PR, 2 * HD), (SLOTS, PR, 2 * HD)).transpose(0, 2, 1).reshape(SR, PR),
        "wk": chunks(np.asarray(L0_xattn_Wk).T),
        "bk": np.asarray(L0_xattn_bk).reshape(DC, P).T,
        "wv": chunks(np.asarray(L0_xattn_Wv).T),
        "bv": np.broadcast_to(np.asarray(L0_xattn_bv)[None, :], (P, D)),
        "wqvk": chunks(L0_attn_Wqvk),
        "wo": chunks(L0_attn_Wo),
        "wgate": chunks(L0_ffn_w_gate),
        "wup": chunks(L0_ffn_w_up),
        "wdown": chunks(L0_ffn_w_down),
        "eye": np.eye(P, dtype=np.float32),
        "headmask": (rows[:, None] // HD == np.arange(HT)[None, :]).astype(np.float32),
        "pairmask": (rows[:SR, None] % 32 // HD == np.arange(2)[None, :]).astype(np.float32),
        "causal": (rows[None, :] > rows[:, None]).astype(np.float32),
    }
    nc = bacc.Bacc("TRN2", target_bir_lowering=False, num_devices=1)
    inputs, args = {}, []
    for name, a in arrays.items():
        a = np.ascontiguousarray(a)
        inputs[f"in_{name}"] = a
        args.append(nc.dram_tensor(f"in_{name}", a.shape, mybir.dt.from_np(a.dtype), kind="ExternalInput").ap())
    out = nc.dram_tensor("out", (Q, D), mybir.dt.float32, kind="ExternalOutput").ap()
    perceiver_layer(nc, *args, out)
    r = run_bass_kernel_spmd(nc, [inputs], core_ids=[0])
    return r.results[0]["out"].reshape(1, Q, D)
```

```python
import concourse.bass as bass
from concourse import mybir
from contextlib import ExitStack

H = 16
HD = 16
D = H * HD
Q = 128
SK = 12544
F = 768
P = 128
DC = D // P
KT = SK // P
T = 7
NB = KT // T
BK = T * P
HK = BK // 2
HT = H // DC
PR = H // 2
SLOTS = 3
SR = SLOTS * 2 * HD
VW = HD + 1
VIA_ACT = (1, 4, 6, 9, 11, 14)
NA = len(VIA_ACT)
ND = H - NA
BUFFER = tuple(h % 3 for h in range(H - 1)) + (1,)
UP = 6
GROUPS = [range(g, min(g + UP, T * PR)) for g in range(0, T * PR, UP)]
UNITS = len(GROUPS)
SLOTS_P = 4
V_TILES = [range(t, min(t + 2, T)) for t in range(0, T, 2)]
NV = len(V_TILES)
PROJECTIONS = (("k", 0, 0), None, ("v", 0), None, ("k", 0, 1), None, ("v", 1), None,
               ("k", 1, 0), None, ("v", 2), None, ("k", 1, 1), None, ("v", 3), None)
MAGIC = 12582912.0
BIG = -float(2 ** 60)
BLOCK = 32
FT = F // P
FH = F // 2


def perceiver_layer(nc: bass.Bass, x_d, ctx_d, maskn_d, maskt_d, wqn_d, wqr_d, bqn_d, bqr_d, wk_d, bk_d, wv_d, bv_d,
                    wqvk_d, wo_d, wgate_d, wup_d, wdown_d, eye_d, headmask_d, pairmask_d, causal_d, out_d):
    f32, f32r, bf16 = mybir.dt.float32, mybir.dt.float32r, mybir.dt.bfloat16
    i32, u8 = mybir.dt.int32, mybir.dt.uint8
    ALU, ACT, AX = mybir.AluOpType, mybir.ActivationFunctionType, mybir.AxisListType

    k_hi_d = nc.dram_tensor("k_hi_scratch", [NB, DC, P, BK], f32, kind="Internal").ap()
    k_lo_d = nc.dram_tensor("k_lo_scratch", [NB, DC, P, BK], f32, kind="Internal").ap()
    v_d = nc.dram_tensor("v_scratch", [NB, P, T * H * VW], f32, kind="Internal").ap()

    with ExitStack() as stack_of_contexts:
        enter = stack_of_contexts.enter_context

        def sb(name, shape, dt=f32):
            return enter(nc.sbuf_tensor(name, shape, dt))

        def sem(name):
            return enter(nc.semaphore(name))

        early = sb("early", [P, 2 * DC * BK + 2 * BK + 2 * T * H * VW])
        ctx_t = early[:, 0:DC * BK]
        staged = early[:, DC * BK:DC * BK + BK].bitcast(bf16).rearrange("p (b k) -> p b k", b=2)
        run_early = early[:, DC * BK + BK:2 * DC * BK].bitcast(bf16).rearrange("p (h k) -> p h k", h=2)
        o1 = 2 * DC * BK
        kf = early[:, o1:o1 + 2 * BK].rearrange("p (m k) -> p m k", m=2)
        o2 = o1 + 2 * BK
        v_new = early[:, o2:o2 + 2 * T * H * VW].rearrange("p (b t h w) -> p b t h w", b=2, t=T, h=H)
        WN = 3 * DC * F
        w_raw = early[:, 0:WN]
        late = early[:, WN:WN + 4096]
        k_hi = sb("k_hi", [P, 2, DC, BK], f32r)
        k_lo = sb("k_lo", [P, DC, BK], f32r)
        k_stack = sb("k_stack", [P, 2, PR, BK], f32r)
        ctx_parts = k_stack[:, 1, :, :].rearrange("p (b c l) k -> p b c l k", b=2, c=2)
        ctx_hi, ctx_lo = ctx_parts[:, :, 0], ctx_parts[:, :, 1]
        middle = sb("middle", [P, 4 * 8 * Q])
        mask_all = middle[:, 0:SK // 4].bitcast(i32)
        probs = [area[:, n * UP * 2 * Q:(n + 1) * UP * 2 * Q] for area in (middle, late) for n in range(2)]
        v_in = sb("v_in", [P, 2 * T * H * VW])
        v_ring = v_in[:, :].rearrange("p (b t h w) -> p b t h w", b=2, t=T, h=H)
        w_kv = v_in[:, 2 * PR * Q:2 * PR * Q + 2 * DC * D]
        q_pad = sb("q_pad", [P, H, Q], f32r)
        q_stack = sb("q_stack", [P, PR, 2, Q], f32r)
        wqr = sb("wqr", [P, DC * PR * SR])
        wqn = sb("wqn", [P, DC, D])
        w_hi = sb("w_hi", [P, 2, DC, D], f32r)
        w_lo = sb("w_lo", [P, 2, DC, D], f32r)
        run_late = sb("run_late", [P, NA - 2, BK], bf16)
        wqvk = sb("wqvk", [P, DC, 3 * D])
        wo = sb("wo", [P, DC, D])
        bqn = sb("bqn", [P, DC])
        bqr = sb("bqr", [P, PR])
        bk = sb("bk", [P, DC])
        bv = sb("bv", [P, D])
        eye = sb("eye", [P, P])
        head_mask = sb("head_mask", [P, HT])
        pair_mask = sb("pair_mask", [P, 2])
        causal = sb("causal", [P, P])
        causal_b = sb("causal_b", [P, P], bf16)
        big_eye = sb("big_eye", [P, P], bf16)
        eye_b = sb("eye_b", [P, P], bf16)
        neg_max = sb("neg_max", [P, H], bf16)
        zeros_b = sb("zeros_b", [P, 512], bf16)
        ones_c = sb("ones_c", [P, 1])
        mask_w = sb("mask_w", [P, 2, BK // 4], i32)
        mask_u = mask_w[:, :, :].rearrange("p b k -> p (b k)").bitcast(u8).rearrange("p (b k) -> p b k", b=2)
        mask_b = sb("mask_b", [P, 2, BK], bf16)
        x0 = sb("x0", [P, D])
        x1 = sb("x1", [P, D])
        x2 = sb("x2", [P, D])
        x3 = sb("x3", [P, D])
        xn = sb("xn", [P, D])
        xt = sb("xt", [P, DC, Q])
        block_max = sb("block_max", [P, 2, H])
        row_max = sb("row_max", [P, H])
        peak = sb("peak", [P, 2])
        stats = sb("stats", [P, 24])
        small = sb("small", [P, 16])
        flag_f = sb("flag_f", [P, 1])
        flag_i = sb("flag_i", [1, 1], i32)
        w_scale = sb("w_scale", [P, WN // BLOCK])
        w_rec = sb("w_rec", [P, WN // BLOCK])

        ps_a = enter(nc.psum_tensor("ps_a", [P, 6, 512], f32))
        ps_k = enter(nc.psum_tensor("ps_k", [P, 512], f32))
        ps_v = enter(nc.psum_tensor("ps_v", [P, 512], f32))
        attended = ps_k[:, :]
        ps_x = ps_a[:, 4, :]
        turn_banks = (ps_v[:, :], ps_a[:, 5, :])

        x_in, eye_in, wqn_in, wqr_in, bq_in, masks_in = (sem(n) for n in ("x_in", "eye_in", "wqn_in", "wqr_in", "bq_in", "masks_in"))
        wkv_in, bk_in, bv_in, mask_all_in, attn_w_in, ffn_w_in = (
            sem(n) for n in ("wkv_in", "bk_in", "bv_in", "mask_all_in", "attn_w_in", "ffn_w_in"))
        ctx_in = sem("ctx_in")
        mask_in = [sem(f"mask_in{i}") for i in range(2)]
        mask_t_in = [sem(f"mask_t_in{i}") for i in range(2)]
        hi_stored = [[sem(f"hi_stored{i}{m}") for m in range(DC)] for i in range(2)]
        lo_stored = [sem(f"lo_stored{m}") for m in range(DC)]
        v_stored = [sem(f"v_stored{i}") for i in range(2)]
        stack_in = [sem(f"stack_in{i}") for i in range(2)]
        v_back = [sem(f"v_back{i}") for i in range(2)]
        out_stored = sem("out_stored")
        consts_set = sem("consts_set")
        ctx_hi_ready, ctx_split, w_split = sem("ctx_hi_ready"), sem("ctx_split"), sem("w_split")
        max_copied, run_taken = sem("max_copied"), sem("run_taken")
        k_projected, k_evacuated, v_projected, v_evacuated = (
            sem(n) for n in ("k_projected", "k_evacuated", "v_projected", "v_evacuated"))
        hi_ready, lo_ready, mask_cast = sem("hi_ready"), sem("lo_ready"), sem("mask_cast")
        max_scored, max_taken = sem("max_scored"), sem("max_taken")
        row_max_ready, max_rows_ready, max_rows_set = sem("row_max_ready"), sem("max_rows_ready"), sem("max_rows_set")
        scored, exp_done, prob_slots_free, sums_done = (
            sem(n) for n in ("scored", "exp_done", "prob_slots_free", "sums_done"))
        sqrt_asked, sqrt_done = sem("sqrt_asked"), sem("sqrt_done")
        q_ready, q_projected, q_copied, q_spread = sem("q_ready"), sem("q_projected"), sem("q_copied"), sem("q_spread")
        normed, transposed, transposed_copied = sem("normed"), sem("transposed"), sem("transposed_copied")
        flag_asked, flag_summed, flag_ready = sem("flag_asked"), sem("flag_summed"), sem("flag_ready")
        sums_copied, sums_turned = sem("sums_copied"), sem("sums_turned")
        weights_ready, weights_turned, weights_copied = sem("weights_ready"), sem("weights_turned"), sem("weights_copied")
        qk_projected, v2_projected, qk_copied, v2_copied = (
            sem(n) for n in ("qk_projected", "v2_projected", "qk_copied", "v2_copied"))
        self_scored, self_shifted, self_exp, probs_turned, probs_copied, self_attended = (
            sem(n) for n in ("self_scored", "self_shifted", "self_exp", "probs_turned", "probs_copied", "self_attended"))
        wv_ready, wv_turned, wv_copied, wo_done = sem("wv_ready"), sem("wv_turned"), sem("wv_copied"), sem("wo_done")
        peak_ready, peak_spread = sem("peak_ready"), sem("peak_spread")
        ffn_projected, gate_ready, sig_ready = sem("ffn_projected"), sem("gate_ready"), sem("sig_ready")
        o_ready, o_turned, o_copied, down_done, result_ready = (
            sem(n) for n in ("o_ready", "o_turned", "o_copied", "down_done", "result_ready"))
        dve_steps, act_steps = sem("dve_steps"), sem("act_steps")

        s_probs = middle[:, 0:H * Q].rearrange("p (h k) -> p h k", h=H)
        s_probs_t = middle[:, H * Q:2 * H * Q].rearrange("p (h q) -> p h q", h=H)
        w_blocks = w_raw.rearrange("p (n b) -> p n b", b=BLOCK)
        up_raw = w_raw[:, 0:DC * F].rearrange("p (t i) -> p t i", t=FT)
        gate_raw = w_raw[:, DC * F:2 * DC * F].rearrange("p (t i) -> p t i", t=FT)
        down_raw = w_raw[:, 2 * DC * F:].rearrange("p (t i) -> p t i", t=DC)
        ffn_wt = v_in[:, 0:2 * DC * F].rearrange("p (w c o) -> p w c o", w=2, c=DC)
        down_wt = wqr[:, 0:FT * D].rearrange("p (t o) -> p t o", t=FT)
        q2_pad = late[:, 0:H * Q].rearrange("p (h q) -> p h q", h=H)
        k2_t = late[:, H * Q:H * Q + DC * Q].rearrange("p (m k) -> p m k", m=DC)
        v2_sb = late[:, 2304:2304 + H * VW].rearrange("p (h w) -> p h w", h=H)
        sums_sb = late[:, 2688:3200]
        both = late[:, 0:2 * F].rearrange("p (w f) -> p w f", w=2)
        up_q, gate_q = both[:, 0, :], both[:, 1, :]
        sig = late[:, 2 * F:3 * F]
        qr = v_in[0:SR, 0:PR * Q].rearrange("p (a q) -> p a q", a=PR)
        qh = v_in[0:SR, PR * Q:2 * PR * Q].rearrange("p (a q) -> p a q", a=PR)
        hidden = late[:, 3 * F:4 * F]
        hidden_t = middle[:, 0:F].rearrange("p (t q) -> p t q", t=FT)

        block = enter(nc.Block())

        @block.sync
        def _(sp):
            sp.dma_start(x0[:], x_d).then_inc(x_in, 16)
            sp.dma_start(w_kv[:, 0:DC * D], wk_d.rearrange("p c n -> p (c n)")).then_inc(wkv_in, 16)
            sp.dma_start(w_kv[:, DC * D:], wv_d.rearrange("p c n -> p (c n)")).then_inc(wkv_in, 16)
            sp.dma_start(ctx_t, ctx_d[0]).then_inc(ctx_in, 16)
            sp.dma_start(eye[:], eye_d).then_inc(eye_in, 16)
            sp.dma_start(wqn[:], wqn_d).then_inc(wqn_in, 16)
            sp.dma_start(bqn[:], bqn_d).then_inc(bq_in, 16)
            sp.dma_start(bqr[0:SR, :], bqr_d).then_inc(bq_in, 16)
            sp.dma_start(head_mask[:], headmask_d).then_inc(masks_in, 16)
            sp.dma_start(pair_mask[0:SR, :], pairmask_d).then_inc(masks_in, 16)
            sp.dma_start(causal[:], causal_d).then_inc(masks_in, 16)
            sp.dma_start(bk[:], bk_d).then_inc(bk_in, 16)
            sp.dma_start(wqr[:, :], wqr_d).then_inc(wqr_in, 16)
            sp.dma_start(mask_all.rearrange("p (b k) -> p b k", b=NB), maskn_d.rearrange("b p k -> p b k")).then_inc(mask_all_in, 16)
            sp.dma_start(mask_w[:, 0, :], maskn_d[0]).then_inc(mask_in[0], 16)
            sp.wait_ge(ctx_split, 1)
            sp.dma_start(ctx_t, ctx_d[1]).then_inc(ctx_in, 16)
            sp.dma_start(mask_w[:, 1, :], maskn_d[1]).then_inc(mask_in[1], 16)
            sp.dma_start(bv[:], bv_d).then_inc(bv_in, 16)
            sp.dma_start(wqvk[:], wqvk_d).then_inc(attn_w_in, 16)
            sp.dma_start(wo[:], wo_d).then_inc(attn_w_in, 16)

            def load(s, par):
                sp.wait_ge(ctx_split, s)
                sp.dma_start(ctx_t, ctx_d[s]).then_inc(ctx_in, 16)
                sp.dma_start(mask_w[:, par, :], maskn_d[s]).then_inc(mask_in[par], 16)

            def store(s, par):
                for m in range(DC):
                    sp.wait_ge(hi_ready, s * DC + m + 1)
                    sp.dma_start(k_hi_d[s, m], k_hi[:, par, m, :].bitcast(f32)).then_inc(hi_stored[par][m], 16)
                    sp.wait_ge(lo_ready, s * DC + m + 1)
                    sp.dma_start(k_lo_d[s, m], k_lo[:, m, :].bitcast(f32)).then_inc(lo_stored[m], 16)
                sp.wait_ge(v_evacuated, s * NV + NV)
                sp.dma_start(v_d[s], v_new[:, par].rearrange("p t h w -> p (t h w)")).then_inc(v_stored[par], 16)

            with sp.Fori(1, NB // 2) as i:
                load(i * 2, 0)
                store(i * 2 - 2, 0)
                load(i * 2 + 1, 1)
                store(i * 2 - 1, 1)

            def load_back(b, par):
                for m in range(DC):
                    for slot in range(SLOTS):
                        src = (k_lo_d if slot == 2 else k_hi_d)[b, m]
                        sp.dma_start(k_stack[slot * 32:slot * 32 + 32, par, m * PR // 2:(m + 1) * PR // 2, :].bitcast(f32),
                                     src.rearrange("(p r) k -> r p k", r=2 * HD)).then_inc(stack_in[par], 16)
                sp.dma_start(v_in[:, par * T * H * VW:(par + 1) * T * H * VW], v_d[b]).then_inc(v_back[par], 16)

            sp.wait_ge(q_spread, 1)
            sp.wait_ge(w_split, 1)
            for b in range(2):
                if b == 1:
                    store(NB - 2, 0)
                    store(NB - 1, 1)
                    sp.wait_ge(v_projected, NB * NV)
                for m in range(DC):
                    sp.wait_ge(hi_stored[b][m], 16)
                    sp.wait_ge(lo_stored[m], 16 * (b + 1))
                sp.wait_ge(v_stored[b], 16)
                load_back(b, b)
            for m in range(DC):
                for par in range(2):
                    sp.wait_ge(hi_stored[par][m], 16 * NB // 2)
                sp.wait_ge(lo_stored[m], 16 * NB)
            for par in range(2):
                sp.wait_ge(v_stored[par], 16 * NB // 2)
            sp.wait_ge(lo_ready, NB * DC)
            sp.wait_ge(row_max_ready, NB + 1)
            sp.dma_start(up_raw, wup_d).then_inc(ffn_w_in, 16)
            sp.dma_start(gate_raw, wgate_d).then_inc(ffn_w_in, 16)
            sp.dma_start(down_raw, wdown_d).then_inc(ffn_w_in, 16)
            with sp.Fori(1, NB // 2) as i:
                for par in range(2):
                    b = i * 2 + par
                    sp.wait_ge(prob_slots_free, (b - 1) * UNITS + SLOTS_P)
                    load_back(b, par)
            sp.wait_ge(out_stored, 16)

        @block.gpsimd
        def _(pool):
            fills = (early[:, o2:],
                     ones_c[:],
                     k_stack[SR:SR + 1, 0, :, :].bitcast(f32))
            for n, fill in enumerate(fills):
                nc.gpsimd.memset(fill, 1.0).then_inc(consts_set, 1)
                pool.wait_ge(consts_set, n + 1)
            nc.gpsimd.memset(zeros_b[:], 0.0).then_inc(consts_set, 1)
            pool.wait_ge(consts_set, 4)

            def split_context(s, par):
                pool.wait_ge(ctx_hi_ready, s + 1)
                nc.gpsimd.tensor_tensor(ctx_lo[:, par].rearrange("p c k -> p (c k)"), ctx_t,
                                        ctx_hi[:, par].rearrange("p c k -> p (c k)").bitcast(f32),
                                        ALU.subtract).then_inc(ctx_split, 1)

            def split(s, par, first, last=False):
                if not last:
                    if not (first and par == 0):
                        pool.wait_ge(lo_ready, s * DC)
                    split_context(s + 1, 1 - par)
                    pool.wait_ge(ctx_split, s + 2)
                if not first:
                    pool.wait_ge(max_scored, (s - 1) * H)
                for m in range(DC):
                    if m or last:
                        pool.wait_ge(lo_ready, s * DC + m)
                    pool.wait_ge(k_evacuated, (s * DC + m + 1) * 2)
                    if not first:
                        pool.wait_ge(hi_stored[par][m], (s - par) * 8)
                    nc.gpsimd.tensor_tensor(k_hi[:, par, m, :], kf[:, m, :], ones_c[:, 0:1].to_broadcast([P, BK]),
                                            ALU.mult).then_inc(hi_ready, 1)
                    pool.wait_ge(hi_ready, s * DC + m + 1)
                    if not (first and par == 0):
                        pool.wait_ge(lo_stored[m], s * 16)
                    nc.gpsimd.tensor_tensor(k_lo[:, m, :], kf[:, m, :], k_hi[:, par, m, :].bitcast(f32),
                                            ALU.subtract).then_inc(lo_ready, 1)

            split_context(0, 0)
            pool.wait_ge(ctx_split, 1)
            split(0, 0, True)
            split(1, 1, True)
            with pool.Fori(1, NB // 2 - 1) as i:
                split(i * 2, 0, False)
                split(i * 2 + 1, 1, False)
            split(NB - 2, 0, False)
            split(NB - 1, 1, False, last=True)
            pool.wait_ge(lo_ready, NB * DC)
            pool.wait_ge(v_projected, NB * NV)
            nc.gpsimd.memset(k_stack[SR:SR + 1, 1, :, :].bitcast(f32), 1.0).then_inc(consts_set, 1)
            pool.wait_ge(mask_cast, NB)
            for b in range(2):
                pool.dma_start(mask_w[:, b, :], maskt_d[b]).then_inc(mask_t_in[b], 16)
            with pool.Fori(1, NB // 2) as i:
                for par in range(2):
                    pool.wait_ge(mask_cast, i * 2 + par + NB - 1)
                    pool.dma_start(mask_w[:, par, :], maskt_d[i * 2 + par]).then_inc(mask_t_in[par], 16)

        @block.scalar
        def _(act):
            steps = [0]

            def link(instruction):
                steps[0] += 1
                instruction.then_inc(act_steps, 1)
                act.wait_ge(act_steps, steps[0])

            def high_context(s, par):
                act.wait_ge(ctx_in, s * 16 + 16)
                nc.scalar.copy(ctx_hi[:, par].rearrange("p c k -> p (c k)"), ctx_t).then_inc(ctx_hi_ready, 1)

            act.wait_ge(sqrt_asked, 1)
            nc.scalar.activation(small[:, 1:2], small[:, 0:1], ACT.Sqrt).then_inc(sqrt_done, 1)
            high_context(0, 0)
            act.wait_ge(bk_in, 16)
            act.wait_ge(consts_set, 1)

            def evacuate_keys(s, m, n, first):
                act.wait_ge(k_projected, (s * DC + m) * 2 + n + 1)
                if not first and n == 0:
                    act.wait_ge(lo_ready, (s - 1) * DC + m + 1)
                nc.scalar.activation(kf[:, m, n * HK:(n + 1) * HK], ps_k[:, 0:HK], ACT.Identity,
                                     bias=bk[:, m:m + 1]).then_inc(k_evacuated, 1)

            def evacuate_values(s, par, k):
                act.wait_ge(v_projected, s * NV + k + 1)
                tiles = V_TILES[k]
                nc.scalar.copy(v_new[:, par, tiles[0]:tiles[-1] + 1, :, 0:HD],
                               ps_v[:, 0:len(tiles) * D].rearrange("p (t h d) -> p t h d", t=len(tiles), h=H)
                               ).then_inc(v_evacuated, 1)

            def copy_scores(s, h):
                k = VIA_ACT.index(h)
                act.wait_ge(max_scored, s * H + h + 1)
                if not (isinstance(s, int) and s == 0 and k < 2):
                    act.wait_ge(run_taken, s * NA + k - 1)
                nc.scalar.copy(staged[:, k % 2, :].rearrange("p (n k) -> p n k", n=2),
                               ps_a[:, 2 * BUFFER[h]:2 * BUFFER[h] + 2, 0:HK]).then_inc(max_copied, 1)

            def evacuate(s, par, first, last=False):
                act.wait_ge(mask_in[par], (s - par) * 8 + 16)
                if not first:
                    act.wait_ge(max_scored, (s - 1) * H)
                nc.scalar.copy(mask_b[:, par, :], mask_u[:, par, :]).then_inc(mask_cast, 1)
                if not last:
                    if not (first and par == 0):
                        act.wait_ge(v_projected, s * NV)
                    high_context(s + 1, 1 - par)
                if not first:
                    act.wait_ge(v_stored[par], (s - par) * 8)
                for slot, work in enumerate(PROJECTIONS):
                    if work and work[0] == "v":
                        evacuate_values(s, par, work[1])
                    if work and work[0] == "k":
                        evacuate_keys(s, work[1], work[2], first and par == 0)
                    if slot in VIA_ACT and not (first and par == 0):
                        copy_scores(s - 1, slot)

            evacuate(0, 0, True)
            evacuate(1, 1, True)
            with act.Fori(1, NB // 2 - 1) as i:
                evacuate(i * 2, 0, False)
                evacuate(i * 2 + 1, 1, False)
            evacuate(NB - 2, 0, False)
            evacuate(NB - 1, 1, False, last=True)
            for h in VIA_ACT:
                copy_scores(NB - 1, h)

            act.wait_ge(max_rows_ready, 1)
            nc.scalar.mul(q_stack[SR:SR + 1, 0:PR // 2, :, :].rearrange("p a b q -> p (a b q)"),
                          ps_a[SR:SR + 1, 0:2, :].rearrange("p a q -> p (a q)"), 1.0).then_inc(max_rows_set, 1)

            for par in range(2):
                act.wait_ge(v_stored[par], 16 * NB // 2)
            with act.Fori(0, NB // 2) as i:
                for u in range(2 * UNITS):
                    n = i * 2 * UNITS + u
                    act.wait_ge(scored, n + 1)
                    act.wait_ge(prob_slots_free, n + 1)
                    width = len(GROUPS[u % UNITS]) * 2 * Q
                    nc.scalar.activation(probs[u % SLOTS_P][:, 0:width],
                                         ps_a[:, 3 * (u % 2):3 * (u % 2) + 3, :].rearrange("p a n -> p (a n)")[:, 0:width],
                                         ACT.Exp).then_inc(exp_done, 1)

            def copy_weights(n, dst):
                act.wait_ge(weights_turned, n + 1)
                nc.scalar.copy(dst, turn_banks[n % 2]).then_inc(weights_copied, 1)

            flat_wt = v_in[:, 0:2 * DC * F]
            for n in range(6):
                copy_weights(n, flat_wt[:, n * 512:(n + 1) * 512])
            for n in range(3):
                copy_weights(6 + n, wqr[:, n * 512:(n + 1) * 512])

            act.wait_ge(sqrt_asked, 2)
            nc.scalar.activation(small[:, 1:2], small[:, 0:1], ACT.Sqrt).then_inc(sqrt_done, 1)
            for g in range(4):
                act.wait_ge(self_shifted, g + 1)
                nc.scalar.activation(s_probs[:, 4 * g:4 * g + 4, :], s_probs[:, 4 * g:4 * g + 4, :], ACT.Exp,
                                     scale=1.0 / D ** 0.5).then_inc(self_exp, 1)
            for g in range(4):
                act.wait_ge(probs_turned, g + 1)
                nc.scalar.copy(s_probs_t[:, 4 * g:4 * g + 4, :].rearrange("p h q -> p (h q)"),
                               turn_banks[g % 2]).then_inc(probs_copied, 1)
            act.wait_ge(sqrt_asked, 3)
            nc.scalar.activation(small[:, 1:2], small[:, 0:1], ACT.Sqrt).then_inc(sqrt_done, 1)
            act.wait_ge(gate_ready, 1)
            nc.scalar.activation(sig, gate_q, ACT.Sigmoid).then_inc(sig_ready, 1)
            act.wait_ge(result_ready, 1)
            act.dma_start(out_d, x3[:]).then_inc(out_stored, 16)

        @block.vector
        def _(dve):
            steps = [0]

            def link(instruction):
                steps[0] += 1
                instruction.then_inc(dve_steps, 1)
                dve.wait_ge(dve_steps, steps[0])

            def layernorm(src, nth):
                link(nc.vector.bn_stats(stats[:, 0:6], src))
                link(nc.vector.bn_aggr(stats[:, 8:10], stats[:, 0:6]))
                nc.vector.tensor_scalar(small[:, 0:1], stats[:, 9:10], 1e-5, None, ALU.add).then_inc(sqrt_asked, 1)
                dve.wait_ge(sqrt_done, nth)
                link(nc.vector.reciprocal(small[:, 3:4], small[:, 1:2]))
                link(nc.vector.tensor_tensor(small[:, 4:5], small[:, 0:1], small[:, 3:4], ALU.mult))
                link(nc.vector.tensor_scalar(small[:, 5:6], small[:, 4:5], small[:, 1:2], 0.5, ALU.add, ALU.mult))
                link(nc.vector.reciprocal(small[:, 6:7], small[:, 5:6]))
                return nc.vector.tensor_scalar(xn[:], src, stats[:, 8:9], small[:, 6:7], ALU.subtract, ALU.mult)

            def copy_turned(nth, psum):
                dve.wait_ge(transposed, nth)
                nc.vector.tensor_copy(xt[:, :, :].rearrange("p c q -> p (c q)"), psum).then_inc(transposed_copied, 1)

            dve.wait_ge(x_in, 16)
            layernorm(x0[:], 1).then_inc(normed, 1)
            dve.wait_ge(wkv_in, 32)
            link(nc.vector.tensor_copy(w_hi[:, :, :, :].rearrange("p w c n -> p (w c n)"), w_kv))
            nc.vector.tensor_tensor(w_lo[:, :, :, :].rearrange("p w c n -> p (w c n)"), w_kv,
                                    w_hi[:, :, :, :].rearrange("p w c n -> p (w c n)").bitcast(f32),
                                    ALU.subtract).then_inc(w_split, 1)
            copy_turned(1, ps_a[:, 0, 0:D])
            dve.wait_ge(eye_in, 16)
            nc.vector.tensor_scalar(big_eye[:], eye[:], BIG, None, ALU.mult)
            nc.vector.tensor_copy(eye_b[:], eye[:])
            dve.wait_ge(bq_in, 32)
            dve.wait_ge(masks_in, 48)
            nc.vector.tensor_copy(causal_b[:], causal[:])
            dve.wait_ge(mask_all_in, 16)
            nc.vector.tensor_reduce(flag_f[:], mask_all, AX.X, ALU.max).then_inc(flag_asked, 1)
            dve.wait_ge(q_projected, 1)
            for m in range(DC):
                link(nc.vector.tensor_scalar(x3[:, m * Q:(m + 1) * Q], ps_a[:, 1, m * Q:(m + 1) * Q], bqn[:, m:m + 1],
                                             HD ** -0.5, ALU.add, ALU.mult))
            for m in range(DC):
                last = nc.vector.tensor_tensor(
                    q_pad[:, m * HT:(m + 1) * HT, :],
                    x3[:, m * Q:(m + 1) * Q].unsqueeze(1).to_broadcast([P, HT, Q]),
                    head_mask[:, :].unsqueeze(2).to_broadcast([P, HT, Q]), ALU.mult)
            last.then_inc(q_ready, 1)
            dve.wait_ge(q_projected, 2)
            link(nc.vector.tensor_scalar(bqr[0:SR, :], bqr[0:SR, :], HD ** -0.5, None, ALU.mult))
            nc.vector.scalar_tensor_tensor(qr, ps_a[0:SR, 2:4, :].rearrange("p a (b q) -> p (a b) q", q=Q), HD ** -0.5,
                                           bqr[0:SR, :].unsqueeze(2).to_broadcast([SR, PR, Q]), ALU.mult,
                                           ALU.add).then_inc(q_copied, 1)
            dve.wait_ge(q_copied, 1)
            for ab in range(2):
                link(nc.vector.tensor_scalar(q_stack[0:SR, :, ab, :], qr, pair_mask[0:SR, ab:ab + 1], None, ALU.mult))
            lo = slice(32, 64)
            for ab in range(2):
                link(nc.vector.tensor_scalar(qh[lo], qr[lo], pair_mask[lo, ab:ab + 1], None, ALU.mult))
                last = nc.vector.tensor_tensor(q_stack[lo, :, ab, :], qh[lo], q_stack[lo, :, ab, :].bitcast(f32), ALU.subtract)
                if ab == 0:
                    link(last)
            last.then_inc(q_spread, 1)
            nc.vector.memset(row_max[:], -3.0e38)
            for tile in (run_early, run_late[:, :, :]):
                nc.vector.memset(tile, -3.0e38)
            dve.wait_ge(flag_summed, 1)
            nc.vector.tensor_scalar(flag_i[0:1, 0:1], ps_v[0:1, 0:1], 0.0, None, ALU.is_gt).then_inc(flag_ready, 1)

            def running(h):
                k = VIA_ACT.index(h)
                return run_early[:, k, :] if k < 2 else run_late[:, k - 2, :]

            def maxima(s, par):
                taken = 0
                for h in range(H):
                    if h in VIA_ACT:
                        k = VIA_ACT.index(h)
                        dve.wait_ge(max_copied, s * NA + k + 1)
                        nc.vector.tensor_tensor(running(h), running(h), staged[:, k % 2, :], ALU.max).then_inc(run_taken, 1)
                        continue
                    dve.wait_ge(max_scored, s * H + h + 1)
                    nc.vector.tensor_reduce(block_max[:, par, taken:taken + 1], ps_a[:, 2 * BUFFER[h]:2 * BUFFER[h] + 2, 0:HK],
                                            AX.XY, ALU.max).then_inc(max_taken, 1)
                    taken += 1
                dve.wait_ge(max_taken, s * ND + ND)
                nc.vector.tensor_tensor(row_max[:, 0:ND], row_max[:, 0:ND], block_max[:, par, 0:ND],
                                        ALU.max).then_inc(row_max_ready, 1)
                dve.wait_ge(row_max_ready, s + 1)
                dve.wait_ge(run_taken, s * NA + NA)

            with dve.Fori(0, NB // 2) as i:
                maxima(i * 2, 0)
                maxima(i * 2 + 1, 1)
            for tiles, at in ((run_early, ND), (run_late[:, :, :], ND + 2)):
                width = BK // 2
                while width >= BK // 8:
                    link(nc.vector.tensor_tensor(tiles[:, :, 0:width], tiles[:, :, 0:width], tiles[:, :, width:2 * width],
                                                 ALU.max))
                    width //= 2
                link(nc.vector.tensor_reduce(row_max[:, at:at + tiles.shape[1]], tiles[:, :, 0:2 * width], AX.X, ALU.max))

            nc.vector.tensor_scalar(neg_max[:], row_max[:], -1.0, None, ALU.mult).then_inc(row_max_ready, 1)
            dve.wait_ge(max_rows_ready, 2)
            nc.vector.tensor_scalar(q_stack[SR:SR + 1, PR // 2:PR, :, :].rearrange("p a b q -> p (a b q)"),
                                    ps_a[SR:SR + 1, 2:4, :].rearrange("p a q -> p (a q)"), 1.0, None,
                                    ALU.mult).then_inc(max_rows_set, 1)

            def cast_mask(par, nth_load, used):
                dve.wait_ge(mask_t_in[par], nth_load)
                dve.wait_ge(scored, used)
                nc.vector.tensor_copy(mask_b[:, par, :], mask_u[:, par, :]).then_inc(mask_cast, 1)

            for b in range(2):
                cast_mask(b, 16, 0)

            dve.wait_ge(ffn_w_in, 48)
            scale_b = w_scale[:, :].unsqueeze(2).to_broadcast([P, WN // BLOCK, BLOCK])
            rec_b = w_rec[:, :].unsqueeze(2).to_broadcast([P, WN // BLOCK, BLOCK])
            link(nc.vector.tensor_reduce(w_scale[:], w_blocks, AX.X, ALU.max, apply_absolute_value=True))
            link(nc.vector.tensor_scalar(w_scale[:], w_scale[:], 1.0 / 7.0, 1e-12, ALU.mult, ALU.max))
            link(nc.vector.reciprocal(w_rec[:], w_scale[:]))
            link(nc.vector.tensor_tensor(w_blocks, w_blocks, rec_b, ALU.mult))
            link(nc.vector.tensor_scalar(w_raw, w_raw, MAGIC, MAGIC, ALU.add, ALU.subtract))
            link(nc.vector.tensor_scalar(w_raw, w_raw, 7.0, -8.0, ALU.min, ALU.max))
            nc.vector.tensor_tensor(w_blocks, w_blocks, scale_b, ALU.mult).then_inc(weights_ready, 1)
            dve.wait_ge(bv_in, 16)
            link(nc.vector.tensor_tensor(x1[:], x0[:], bv[:], ALU.add))

            with dve.Fori(1, NB // 2) as i:
                for par in range(2):
                    cast_mask(par, i * 16 + 16, (i * 2 + par - 1) * UNITS)

            dve.wait_ge(sums_done, 1)
            nc.vector.tensor_copy(sums_sb, attended).then_inc(sums_copied, 1)
            dve.wait_ge(sums_turned, 1)
            turned = ps_x.rearrange("p (h r) -> p h r", r=32)
            link(nc.vector.reciprocal(stats[:, 0:H], turned[:, :, HD]))
            link(nc.vector.tensor_tensor(xn[:, :].rearrange("p (h d) -> p h d", h=H), turned[:, :, 0:HD],
                                         stats[:, 0:H].unsqueeze(2).to_broadcast([P, H, HD]), ALU.mult))
            link(nc.vector.tensor_tensor(x1[:], x1[:], xn[:], ALU.add))

            layernorm(x1[:], 2).then_inc(normed, 1)
            copy_turned(2, ps_k[:, 0:D])
            dve.wait_ge(qk_projected, 1)
            nc.vector.tensor_copy(x3[:], ps_x[:, 0:D])
            link(nc.vector.tensor_copy(k2_t.rearrange("p m k -> p (m k)"), ps_x[:, D:2 * D]))
            for m in range(DC):
                last = nc.vector.tensor_tensor(
                    q2_pad[:, m * HT:(m + 1) * HT, :],
                    x3[:, m * Q:(m + 1) * Q].unsqueeze(1).to_broadcast([P, HT, Q]),
                    head_mask[:, :].unsqueeze(2).to_broadcast([P, HT, Q]), ALU.mult)
            last.then_inc(qk_copied, 1)
            dve.wait_ge(v2_projected, 1)
            nc.vector.memset(v2_sb[:, :, HD:VW], 1.0)
            nc.vector.tensor_copy(v2_sb[:, :, 0:HD], ps_k[:, D:2 * D].rearrange("p (h d) -> p h d", h=H)).then_inc(v2_copied, 1)
            for g in range(4):
                dve.wait_ge(self_scored, g + 1)
                scores = ps_a[:, g, :].rearrange("p (h k) -> p h k", h=4)
                link(nc.vector.tensor_reduce(block_max[:, 0, 4 * g:4 * g + 4], scores, AX.X, ALU.max))
                nc.vector.tensor_tensor(s_probs[:, 4 * g:4 * g + 4, :], scores,
                                        block_max[:, 0, 4 * g:4 * g + 4].unsqueeze(2).to_broadcast([P, 4, Q]),
                                        ALU.subtract).then_inc(self_shifted, 1)
            dve.wait_ge(self_attended, 1)
            summed = ps_x[:, 0:H * VW].rearrange("p (h w) -> p h w", h=H)
            link(nc.vector.reciprocal(stats[:, 0:H], summed[:, :, HD]))
            nc.vector.tensor_tensor(xn[:, :].rearrange("p (h d) -> p h d", h=H), summed[:, :, 0:HD],
                                    stats[:, 0:H].unsqueeze(2).to_broadcast([P, H, HD]), ALU.mult).then_inc(wv_ready, 1)
            dve.wait_ge(wv_turned, 1)
            nc.vector.tensor_copy(xt[:, :, :].rearrange("p c q -> p (c q)"), ps_k[:, 0:D]).then_inc(wv_copied, 1)
            dve.wait_ge(wo_done, 1)
            link(nc.vector.tensor_tensor(x2[:], ps_x[:, 0:D], x1[:], ALU.add))

            def peaks(views, nth):
                for n, view in enumerate(views):
                    last = nc.vector.tensor_reduce(peak[:, n:n + 1], view,
                                                   AX.XY if len(view.shape) == 3 else AX.X, ALU.max, apply_absolute_value=True)
                last.then_inc(peak_ready, 1)
                dve.wait_ge(peak_spread, nth)
                link(nc.vector.tensor_reduce(small[:, 8:8 + len(views)],
                                             ps_x[:, 0:len(views) * P].rearrange("p (n k) -> p n k", k=P), AX.X, ALU.max))
                link(nc.vector.tensor_scalar(small[:, 8:8 + len(views)], small[:, 8:8 + len(views)], 1.0 / 32767.0, 1e-12,
                                             ALU.mult, ALU.max))
                link(nc.vector.reciprocal(small[:, 10:10 + len(views)], small[:, 8:8 + len(views)]))

            def quantise(dst, src, n):
                link(nc.vector.tensor_scalar(dst, src, small[:, 10 + n:11 + n], MAGIC, ALU.mult, ALU.add))
                link(nc.vector.tensor_scalar(dst, dst, MAGIC, 32767.0, ALU.subtract, ALU.min))
                return nc.vector.tensor_scalar(dst, dst, -32768.0, small[:, 8 + n:9 + n], ALU.max, ALU.mult)

            link(layernorm(x2[:], 3))
            peaks([xn[:]], 1)
            quantise(xn[:], xn[:], 0).then_inc(normed, 1)
            copy_turned(3, ps_k[:, 0:D])
            dve.wait_ge(ffn_projected, 1)
            up_ps, gate_ps = ps_a[:, 0:2, 0:FH], ps_a[:, 2:4, 0:FH]
            peaks([up_ps, gate_ps], 2)
            quantise(gate_q.rearrange("p (n f) -> p n f", n=2), gate_ps, 1).then_inc(gate_ready, 1)
            link(quantise(up_q.rearrange("p (n f) -> p n f", n=2), up_ps, 0))
            dve.wait_ge(sig_ready, 1)
            link(nc.vector.tensor_scalar(sig, sig, 65536.0, MAGIC, ALU.mult, ALU.add))
            link(nc.vector.tensor_scalar(sig, sig, MAGIC, 0.0, ALU.subtract, ALU.max))
            link(nc.vector.tensor_scalar(sig, sig, 65535.0, 1.0 / 65536.0, ALU.min, ALU.mult))
            link(nc.vector.tensor_tensor(hidden, gate_q, sig, ALU.mult))
            peaks([hidden], 3)
            link(quantise(hidden, hidden, 0))
            link(nc.vector.tensor_tensor(hidden, hidden, up_q, ALU.mult))
            peaks([hidden], 4)
            quantise(hidden, hidden, 0).then_inc(o_ready, 1)
            for n in range(2):
                dve.wait_ge(o_turned, n + 1)
                nc.vector.tensor_copy(hidden_t[:, 3 * n:3 * n + 3, :].rearrange("p t q -> p (t q)"),
                                      turn_banks[n][:, 0:3 * Q]).then_inc(o_copied, 1)
            dve.wait_ge(down_done, 1)
            nc.vector.tensor_tensor(x3[:], ps_k[:, 0:D], x2[:], ALU.add).then_inc(result_ready, 1)

        @block.tensor
        def _(pe):
            part_pairs = ((w_hi, ctx_hi), (w_hi, ctx_lo), (w_lo, ctx_hi))
            terms = [(w, part, c) for w, part in part_pairs for c in range(DC)]

            def project_keys(s, par, m, n):
                if not (isinstance(s, int) and s == 0 and m == 0 and n == 0):
                    pe.wait_ge(k_evacuated, (s * DC + m) * 2 + n)
                for k, (w, part, c) in enumerate(terms):
                    last = nc.tensor.matmul(ps_k[:, 0:HK], w[:, 0, c, m * P:(m + 1) * P],
                                            part[:, par, c, n * HK:(n + 1) * HK], start=(k == 0), stop=(k == len(terms) - 1))
                last.then_inc(k_projected, 1)

            def project_values(s, par, k):
                if not (isinstance(s, int) and s == 0 and k == 0):
                    pe.wait_ge(v_evacuated, s * NV + k)
                for n, t in enumerate(V_TILES[k]):
                    for j, (w, part, c) in enumerate(terms):
                        last = nc.tensor.matmul(ps_v[:, n * D:(n + 1) * D], part[:, par, c, t * P:(t + 1) * P],
                                                w[:, 1, c, :], start=(j == 0), stop=(j == len(terms) - 1))
                last.then_inc(v_projected, 1)

            def project(s, par, slot):
                work = PROJECTIONS[slot]
                if work is None:
                    return
                if work[0] == "k":
                    project_keys(s, par, *work[1:])
                else:
                    project_values(s, par, work[1])

            def score_for_max(s, par, h, masked):
                m = h // HT
                if h % HT == 0:
                    pe.wait_ge(hi_ready, s * DC + m + 1)
                if h == 0 and masked:
                    pe.wait_ge(mask_cast, s + 1)
                earlier = [a for a in range(h) if BUFFER[a] == BUFFER[h]]
                before = earlier[-1] if earlier else max(a for a in range(H) if BUFFER[a] == BUFFER[h])
                back = 0 if earlier else 1
                if not (isinstance(s, int) and s == 0 and back):
                    if before in VIA_ACT:
                        pe.wait_ge(max_copied, (s - back) * NA + VIA_ACT.index(before) + 1)
                    else:
                        rank = before - sum(a < before for a in VIA_ACT)
                        pe.wait_ge(max_taken, (s - back) * ND + rank + 1)
                for n in range(2):
                    out = ps_a[:, 2 * BUFFER[h] + n, 0:HK]
                    last = nc.tensor.matmul(out, q_pad[:, h, :], k_hi[:, par, m, n * HK:(n + 1) * HK],
                                            start=True, stop=not masked)
                    if masked:
                        last = nc.tensor.matmul(out, big_eye[:], mask_b[:, par, n * HK:(n + 1) * HK], start=False, stop=True)
                last.then_inc(max_scored, 1)

            pe.wait_ge(normed, 1)
            pe.wait_ge(eye_in, 16)
            for c in range(DC):
                last = nc.tensor.transpose(ps_a[:, 0, c * Q:(c + 1) * Q], xn[:, c * P:(c + 1) * P], eye[:])
            last.then_inc(transposed, 1)
            pe.wait_ge(transposed_copied, 1)
            pe.wait_ge(wqn_in, 16)
            for m in range(DC):
                for c in range(DC):
                    last = nc.tensor.matmul(ps_a[:, 1, m * Q:(m + 1) * Q], wqn[:, c, m * P:(m + 1) * P], xt[:, c, :],
                                            start=(c == 0), stop=(c == DC - 1))
            last.then_inc(q_projected, 1)
            pe.wait_ge(wqr_in, 16)
            wqr_v = wqr[:, :].rearrange("p (c a r) -> p c a r", c=DC, a=PR)
            for a in range(PR):
                for c in range(DC):
                    last = nc.tensor.matmul(ps_a[0:SR, 2 + a // 4, (a % 4) * Q:(a % 4 + 1) * Q], wqr_v[:, c, a, :], xt[:, c, :],
                                            start=(c == 0), stop=(c == DC - 1))
            last.then_inc(q_projected, 1)
            pe.wait_ge(w_split, 1)
            pe.wait_ge(ctx_split, 1)
            for slot in range(H):
                project(0, 0, slot)
            pe.wait_ge(flag_asked, 1)
            pe.wait_ge(consts_set, 4)
            pe.wait_ge(v_evacuated, NV)
            nc.tensor.matmul(ps_v[0:1, 0:1], flag_f[:], ones_c[:], start=True, stop=True).then_inc(flag_summed, 1)
            pe.wait_ge(flag_ready, 1)
            masked_flag = pe.value_load(flag_i[0:1, 0:1], min_val=0, max_val=1)

            def attend(masked):
                pe.wait_ge(q_ready, 1)
                pe.wait_ge(q_copied, 1)

                def step(s, par):
                    pe.wait_ge(ctx_split, s + 1)
                    for slot in range(H):
                        project(s, par, slot)
                        score_for_max(s - 1, 1 - par, slot, masked)

                step(1, 1)
                with pe.Fori(1, NB // 2) as i:
                    step(i * 2, 0)
                    step(i * 2 + 1, 1)
                for h in range(H):
                    score_for_max(NB - 1, 1, h, masked)

                pe.wait_ge(row_max_ready, NB + 1)
                columns = [h for h in range(H) if h not in VIA_ACT] + list(VIA_ACT)
                for h in range(H):
                    last = nc.tensor.matmul(ps_a[SR:SR + 1, h // 4, (h % 4) * Q:(h % 4 + 1) * Q], neg_max[:, columns.index(h):columns.index(h) + 1], eye_b[:],
                                            start=True, stop=True)
                    if h % HT == HT - 1:
                        last.then_inc(max_rows_ready, 1)

                pe.wait_ge(k_evacuated, NB * DC * 2)
                nc.tensor.matmul(attended, zeros_b[:, 0:P], zeros_b[:], start=True, stop=True,
                                 skip_group_check=True).then_inc(prob_slots_free, SLOTS_P)
                pe.wait_ge(max_rows_set, 2)
                pe.wait_ge(q_spread, 1)
                pe.wait_ge(consts_set, 5)

                def score(b_par, u):
                    for k, g in enumerate(GROUPS[u]):
                        t, a = divmod(g, PR)
                        bank = 3 * (u % 2) + k // 2
                        last = nc.tensor.matmul(ps_a[:, bank, (k % 2) * 2 * Q:(k % 2 + 1) * 2 * Q],
                                                k_stack[0:SR + 1, b_par, a, t * P:(t + 1) * P],
                                                q_stack[0:SR + 1, a, :, :].rearrange("p b q -> p (b q)"),
                                                start=(k % 2 == 0), stop=(k % 2 == 1) and not masked, skip_group_check=True)
                        if masked and k % 2 == 1:
                            last = nc.tensor.matmul(ps_a[:, bank, :], big_eye[:],
                                                    mask_b[:, b_par, t * P:(t + 1) * P].unsqueeze(1).to_broadcast([P, 4, Q]),
                                                    start=False, stop=True, skip_group_check=True)
                    last.then_inc(scored, 1)

                def add_up(b_par, u, slot):
                    for k in range(2 * len(GROUPS[u])):
                        t, h = divmod(2 * GROUPS[u][0] + k, H)
                        j, c = h % 4, h // 4
                        last = nc.tensor.matmul(attended[32 * j:32 * j + VW, c * Q:(c + 1) * Q], v_ring[:, b_par, t, h, :],
                                                probs[slot][:, k * Q:(k + 1) * Q], start=False, stop=False,
                                                skip_group_check=True)
                    last.then_inc(prob_slots_free, 1)

                def arrive(b, par):
                    pe.wait_ge(stack_in[par], (b - par) * 48 + 96)
                    if masked:
                        pe.wait_ge(mask_cast, b + NB + 1)

                def two_blocks(i, final):
                    for u in range(2 * UNITS):
                        n = i * (2 * UNITS) + u
                        pe.wait_ge(exp_done, n + 1)
                        if not (final and u >= 2 * UNITS - 2):
                            nxt = (u + 2) % (2 * UNITS)
                            if nxt == 0:
                                arrive(i * 2 + 2, 0)
                            if nxt == UNITS:
                                arrive(i * 2 + 1, 1)
                            score(nxt // UNITS, nxt % UNITS)
                        if u % UNITS == 0:
                            pe.wait_ge(v_back[u // UNITS], i * 16 + 16)
                        add_up(u // UNITS, u % UNITS, u % SLOTS_P)

                arrive(0, 0)
                score(0, 0)
                score(0, 1)
                with pe.Fori(0, NB // 2 - 1) as i:
                    two_blocks(i, False)
                two_blocks(NB // 2 - 1, True)

            for masked in (False, True):
                with pe.If(masked_flag == int(masked)):
                    attend(masked)

            nc.tensor.matmul(ps_v[0:1, 0:1], zeros_b[:, 0:1], zeros_b[:, 0:1], start=True, stop=True).then_inc(sums_done, 1)
            pe.wait_ge(sums_copied, 1)
            for c in range(4):
                last = nc.tensor.transpose(ps_x[:, c * P:(c + 1) * P], sums_sb[:, c * P:(c + 1) * P], eye[:])
            last.then_inc(sums_turned, 1)

            pe.wait_ge(weights_ready, 1)
            tiles = [(raw, t, c) for raw in (up_raw, gate_raw) for c in range(DC) for t in range(FT)]
            tiles += [(down_raw, o, t) for t in range(FT) for o in range(DC)]
            for n, (raw, t, c) in enumerate(tiles):
                group = n // 4
                if n % 4 == 0 and group >= 2:
                    pe.wait_ge(weights_copied, group - 1)
                last = nc.tensor.transpose(turn_banks[group % 2][:, (n % 4) * P:(n % 4 + 1) * P], raw[:, t, c * P:(c + 1) * P], eye[:])
                if n % 4 == 3:
                    last.then_inc(weights_turned, 1)

            def turn_rows(nth):
                pe.wait_ge(normed, nth)
                for c in range(DC):
                    last = nc.tensor.transpose(ps_k[:, c * Q:(c + 1) * Q], xn[:, c * P:(c + 1) * P], eye[:])
                last.then_inc(transposed, 1)
                pe.wait_ge(transposed_copied, nth)

            turn_rows(2)
            pe.wait_ge(attn_w_in, 32)
            for n, at in enumerate((0, P, 2 * D, 2 * D + P)):
                for c in range(DC):
                    last = nc.tensor.matmul(ps_x[:, n * Q:(n + 1) * Q], wqvk[:, c, at:at + P], xt[:, c, :],
                                            start=(c == 0), stop=(c == DC - 1))
            last.then_inc(qk_projected, 1)
            for c in range(DC):
                last = nc.tensor.matmul(ps_k[:, D:2 * D], xt[:, c, :], wqvk[:, c, D:2 * D], start=(c == 0), stop=(c == DC - 1))
            last.then_inc(v2_projected, 1)
            pe.wait_ge(qk_copied, 1)
            for g in range(4):
                for k in range(4):
                    h = 4 * g + k
                    nc.tensor.matmul(ps_a[:, g, k * Q:(k + 1) * Q], q2_pad[:, h, :], k2_t[:, h // HT, :], start=(k == 0),
                                     stop=False, skip_group_check=True)
                nc.tensor.matmul(ps_a[:, g, :], big_eye[:], causal_b[:, :].unsqueeze(1).to_broadcast([P, 4, Q]),
                                 start=False, stop=True, skip_group_check=True).then_inc(self_scored, 1)
            pe.wait_ge(weights_copied, 9)
            pe.wait_ge(v2_copied, 1)

            def attend_self(g):
                pe.wait_ge(probs_copied, g + 1)
                for k in range(4):
                    h = 4 * g + k
                    last = nc.tensor.matmul(ps_x[:, h * VW:(h + 1) * VW], s_probs_t[:, h, :], v2_sb[:, h, :],
                                            start=True, stop=True, skip_group_check=True)
                return last

            for g in range(4):
                pe.wait_ge(self_exp, g + 1)
                if g >= 2:
                    attend_self(g - 2)
                for k in range(4):
                    last = nc.tensor.transpose(turn_banks[g % 2][:, k * P:(k + 1) * P], s_probs[:, 4 * g + k, :], eye[:])
                last.then_inc(probs_turned, 1)
            attend_self(2)
            attend_self(3).then_inc(self_attended, 1)
            pe.wait_ge(wv_ready, 1)
            for c in range(DC):
                last = nc.tensor.transpose(ps_k[:, c * Q:(c + 1) * Q], xn[:, c * P:(c + 1) * P], eye[:])
            last.then_inc(wv_turned, 1)
            pe.wait_ge(wv_copied, 1)
            for c in range(DC):
                last = nc.tensor.matmul(ps_x[:, 0:D], xt[:, c, :], wo[:, c, :], start=(c == 0), stop=(c == DC - 1))
            last.then_inc(wo_done, 1)

            def spread_peaks(nth, count):
                pe.wait_ge(peak_ready, nth)
                for n in range(count):
                    last = nc.tensor.matmul(ps_x[:, n * P:(n + 1) * P], peak[:, n:n + 1].to_broadcast([P, P]), eye[:],
                                            start=True, stop=True)
                last.then_inc(peak_spread, 1)

            spread_peaks(1, 1)
            turn_rows(3)
            for w in range(2):
                for n in range(2):
                    for c in range(DC):
                        last = nc.tensor.matmul(ps_a[:, 2 * w + n, 0:FH], xt[:, c, :], ffn_wt[:, w, c, n * FH:(n + 1) * FH],
                                                start=(c == 0), stop=(c == DC - 1))
            last.then_inc(ffn_projected, 1)
            spread_peaks(2, 2)
            spread_peaks(3, 1)
            spread_peaks(4, 1)
            pe.wait_ge(o_ready, 1)
            for t in range(FT):
                last = nc.tensor.transpose(turn_banks[t // 3][:, (t % 3) * Q:(t % 3 + 1) * Q], hidden[:, t * P:(t + 1) * P], eye[:])
                if t % 3 == 2:
                    last.then_inc(o_turned, 1)
            for t in range(FT):
                if t % 3 == 0:
                    pe.wait_ge(o_copied, t // 3 + 1)
                last = nc.tensor.matmul(ps_k[:, 0:D], hidden_t[:, t, :], down_wt[:, t, :], start=(t == 0), stop=(t == FT - 1))
            last.then_inc(down_done, 1)


def kernel(x, ctx_1024, mask_BxSxS2_bf0, L0_xattn_Wq, L0_xattn_bq, L0_xattn_Wk, L0_xattn_bk, L0_xattn_Wv, L0_xattn_bv,
           L0_attn_Wqvk, L0_attn_Wo, L0_ffn_w_gate, L0_ffn_w_up, L0_ffn_w_down):
    import numpy as np
    import concourse.bacc as bacc
    from concourse.bass_utils import run_bass_kernel_spmd

    def chunks(w):
        return np.ascontiguousarray(np.asarray(w).reshape(-1, P, np.asarray(w).shape[1]).transpose(1, 0, 2))

    def words(a):
        return np.ascontiguousarray(a).view(np.int32)

    mask = np.asarray(mask_BxSxS2_bf0)[0].view(np.uint8)
    wq_t = chunks(np.asarray(L0_xattn_Wq).T)
    rows = np.arange(P)
    arrays = {
        "x": np.asarray(x)[0],
        "ctx": np.asarray(ctx_1024)[0].T.reshape(DC, P, NB, BK).transpose(2, 1, 0, 3),
        "maskn": words(mask.reshape(Q, NB, BK).transpose(1, 0, 2)),
        "maskt": words(mask.T.reshape(NB, T, P, Q).transpose(0, 2, 1, 3).reshape(NB, P, T * Q)),
        "wqn": wq_t,
        "wqr": np.broadcast_to(wq_t.reshape(P, DC, PR, 1, 2 * HD), (P, DC, PR, SLOTS, 2 * HD)).reshape(P, DC * PR * SR),
        "bqn": np.asarray(L0_xattn_bq).reshape(DC, P).T,
        "bqr": np.broadcast_to(np.asarray(L0_xattn_bq).reshape(1, PR, 2 * HD), (SLOTS, PR, 2 * HD)).transpose(0, 2, 1).reshape(SR, PR),
        "wk": chunks(np.asarray(L0_xattn_Wk).T),
        "bk": np.asarray(L0_xattn_bk).reshape(DC, P).T,
        "wv": chunks(np.asarray(L0_xattn_Wv).T),
        "bv": np.broadcast_to(np.asarray(L0_xattn_bv)[None, :], (P, D)),
        "wqvk": chunks(L0_attn_Wqvk),
        "wo": chunks(L0_attn_Wo),
        "wgate": chunks(L0_ffn_w_gate),
        "wup": chunks(L0_ffn_w_up),
        "wdown": chunks(L0_ffn_w_down),
        "eye": np.eye(P, dtype=np.float32),
        "headmask": (rows[:, None] // HD == np.arange(HT)[None, :]).astype(np.float32),
        "pairmask": (rows[:SR, None] % 32 // HD == np.arange(2)[None, :]).astype(np.float32),
        "causal": (rows[None, :] > rows[:, None]).astype(np.float32),
    }
    nc = bacc.Bacc("TRN2", target_bir_lowering=False, num_devices=1)
    inputs, args = {}, []
    for name, a in arrays.items():
        a = np.ascontiguousarray(a)
        inputs[f"in_{name}"] = a
        args.append(nc.dram_tensor(f"in_{name}", a.shape, mybir.dt.from_np(a.dtype), kind="ExternalInput").ap())
    out = nc.dram_tensor("out", (Q, D), mybir.dt.float32, kind="ExternalOutput").ap()
    perceiver_layer(nc, *args, out)
    r = run_bass_kernel_spmd(nc, [inputs], core_ids=[0])
    return r.results[0]["out"].reshape(1, Q, D)
```

```python
import concourse.bass as bass
from concourse import mybir
from contextlib import ExitStack

H = 16
HD = 16
D = H * HD
Q = 128
SK = 12544
F = 768
P = 128
DC = D // P
KT = SK // P
T = 7
NB = KT // T
BK = T * P
HK = BK // 2
HT = H // DC
PR = H // 2
SLOTS = 3
SR = SLOTS * 2 * HD
VW = HD + 1
VIA_ACT = (1, 3, 5, 10, 12, 15)
NA = len(VIA_ACT)
ND = H - NA
BUFFER = [[(par * H + h) % 3 for h in range(H)] for par in range(2)]
UP = 6
GROUPS = [range(g, min(g + UP, T * PR)) for g in range(0, T * PR, UP)]
UNITS = len(GROUPS)
SLOTS_P = 4
V_TILES = [range(t, min(t + 2, T)) for t in range(0, T, 2)]
NV = len(V_TILES)
PROJECTIONS = (("k", 0, 0), None, ("v", 0), None, ("k", 0, 1), None, ("v", 1), None,
               ("k", 1, 0), None, ("v", 2), None, ("k", 1, 1), None, ("v", 3), None)
ROOT_GUESS = 1597463007.0
LEAST = -3.0e38
MAGIC = 12582912.0
BIG = -float(2 ** 60)
BLOCK = 32
FT = F // P
FH = F // 2
LAG = H // 2
PREPARE_SLOTS = (5, 3)
WARM_FIRST = 14
WARM = (15, 13, 8, 10, 14, 18, 6, 2)


def perceiver_layer(nc: bass.Bass, x_d, ctx_d, maskn_d, maskt_d, wqn_d, wqr_d, bqn_d, bqr_d, wk_d, bk_d, wv_d, bv_d,
                    wqvk_d, wo_d, wgate_d, wup_d, wdown_d, eye_d, headmask_d, pairmask_d, causal_d, out_d):
    f32, f32r, bf16 = mybir.dt.float32, mybir.dt.float32r, mybir.dt.bfloat16
    i32, u8 = mybir.dt.int32, mybir.dt.uint8
    ALU, ACT, AX = mybir.AluOpType, mybir.ActivationFunctionType, mybir.AxisListType

    k_hi_d = nc.dram_tensor("k_hi_scratch", [NB, DC, P, BK], f32, kind="Internal").ap()
    k_lo_d = nc.dram_tensor("k_lo_scratch", [NB, DC, P, BK], f32, kind="Internal").ap()
    v_d = nc.dram_tensor("v_scratch", [NB, P, T * H * VW], f32, kind="Internal").ap()

    with ExitStack() as stack_of_contexts:
        enter = stack_of_contexts.enter_context

        def sb(name, shape, dt=f32):
            return enter(nc.sbuf_tensor(name, shape, dt))

        def sem(name):
            return enter(nc.semaphore(name))

        early = sb("early", [P, 2 * DC * BK + 2 * BK + 2 * T * H * VW])
        ctx_t = early[:, 0:DC * BK]
        staged = early[:, DC * BK:DC * BK + BK].bitcast(bf16).rearrange("p (b k) -> p b k", b=2)
        run_early = early[:, DC * BK + BK:2 * DC * BK].bitcast(bf16).rearrange("p (h k) -> p h k", h=2)
        o1 = 2 * DC * BK
        kf = early[:, o1:o1 + 2 * BK].rearrange("p (m k) -> p m k", m=2)
        o2 = o1 + 2 * BK
        v_new = early[:, o2:o2 + 2 * T * H * VW].rearrange("p (b t h w) -> p b t h w", b=2, t=T, h=H)
        WN = 3 * DC * F
        w_raw = early[:, 0:WN]
        late = early[:, WN:WN + 4096]
        k_hi = sb("k_hi", [P, 2, DC, BK], f32r)
        k_lo = sb("k_lo", [P, DC, BK], f32r)
        k_stack = sb("k_stack", [P, 2, PR, BK], f32r)
        ctx_parts = k_stack[:, 1, :, :].rearrange("p (b c l) k -> p b c l k", b=2, c=2)
        ctx_hi, ctx_lo = ctx_parts[:, :, 0], ctx_parts[:, :, 1]
        middle = sb("middle", [P, 4 * 8 * Q])
        mask_all = middle[:, 0:SK // 4].bitcast(i32)
        probs = [area[:, n * UP * 2 * Q:(n + 1) * UP * 2 * Q] for area in (middle, late) for n in range(2)]
        v_in = sb("v_in", [P, 2 * T * H * VW])
        v_ring = v_in[:, :].rearrange("p (b t h w) -> p b t h w", b=2, t=T, h=H)
        w_kv = v_in[:, 2 * PR * Q:2 * PR * Q + 2 * DC * D]
        q_pad = sb("q_pad", [P, H, Q], f32r)
        q_stack = sb("q_stack", [P, PR, 2, Q], f32r)
        wqr = sb("wqr", [P, DC * PR * SR])
        wqn = sb("wqn", [P, DC, D])
        w_hi = sb("w_hi", [P, 2, DC, D], f32r)
        w_lo = sb("w_lo", [P, 2, DC, D], f32r)
        run_late = sb("run_late", [P, NA - 2, BK], bf16)
        wqvk = sb("wqvk", [P, DC, 3 * D])
        wo = sb("wo", [P, DC, D])
        bqn = sb("bqn", [P, DC])
        bqr = sb("bqr", [P, PR])
        bk = sb("bk", [P, DC])
        bv = sb("bv", [P, D])
        eye = sb("eye", [P, P])
        head_mask = sb("head_mask", [P, HT])
        pair_mask = sb("pair_mask", [P, 2])
        causal = sb("causal", [P, P])
        causal_b = sb("causal_b", [P, P], bf16)
        big_eye = sb("big_eye", [P, P], bf16)
        eye_b = sb("eye_b", [P, P], bf16)
        neg_max = sb("neg_max", [P, H], bf16)
        zeros_b = sb("zeros_b", [P, 512], bf16)
        ones_c = sb("ones_c", [P, 1])
        mask_w = sb("mask_w", [P, 2, BK // 4], i32)
        mask_u = mask_w[:, :, :].rearrange("p b k -> p (b k)").bitcast(u8).rearrange("p (b k) -> p b k", b=2)
        mask_b = sb("mask_b", [P, 2, BK], bf16)
        x0 = sb("x0", [P, D])
        x1 = sb("x1", [P, D])
        x2 = sb("x2", [P, D])
        x3 = sb("x3", [P, D])
        xn = sb("xn", [P, D])
        xt = sb("xt", [P, DC, Q])
        block_max = sb("block_max", [P, 2, H])
        row_max = sb("row_max", [P, H])
        peak = sb("peak", [P, 2])
        stats = sb("stats", [P, 24])
        small = sb("small", [P, 16])
        magic = sb("magic", [P, 2])
        flag_f = sb("flag_f", [P, 1])
        flag_i = sb("flag_i", [1, 1], i32)
        w_scale = sb("w_scale", [P, WN // BLOCK])
        w_rec = sb("w_rec", [P, WN // BLOCK])

        ps_a = enter(nc.psum_tensor("ps_a", [P, 6, 512], f32))
        ps_k = enter(nc.psum_tensor("ps_k", [P, 512], f32))
        ps_v = enter(nc.psum_tensor("ps_v", [P, 512], f32))
        attended = ps_k[:, :]
        ps_x = ps_a[:, 4, :]
        turn_banks = (ps_v[:, :], ps_a[:, 5, :], ps_k[:, :], ps_a[:, 0, :])

        x_in, eye_in, wqn_in, wqr_in, bq_in, masks_in = (sem(n) for n in ("x_in", "eye_in", "wqn_in", "wqr_in", "bq_in", "masks_in"))
        wkv_in, bk_in, bv_in, mask_all_in, attn_w_in, ffn_w_in = (
            sem(n) for n in ("wkv_in", "bk_in", "bv_in", "mask_all_in", "attn_w_in", "ffn_w_in"))
        ctx_in = sem("ctx_in")
        mask_in = [sem(f"mask_in{i}") for i in range(2)]
        mask_t_in = [sem(f"mask_t_in{i}") for i in range(2)]
        hi_stored = [[sem(f"hi_stored{i}{m}") for m in range(DC)] for i in range(2)]
        lo_stored = [sem(f"lo_stored{m}") for m in range(DC)]
        v_stored = [sem(f"v_stored{i}") for i in range(2)]
        stack_in = [sem(f"stack_in{i}") for i in range(2)]
        v_back = [sem(f"v_back{i}") for i in range(2)]
        out_stored = sem("out_stored")
        consts_set = sem("consts_set")
        ctx_hi_ready, ctx_split, w_split = sem("ctx_hi_ready"), sem("ctx_split"), sem("w_split")
        max_copied, run_taken = sem("max_copied"), sem("run_taken")
        k_projected, k_evacuated, v_projected, v_evacuated = (
            sem(n) for n in ("k_projected", "k_evacuated", "v_projected", "v_evacuated"))
        hi_ready, lo_ready, mask_cast = sem("hi_ready"), sem("lo_ready"), sem("mask_cast")
        max_scored, max_taken = sem("max_scored"), sem("max_taken")
        row_max_ready, max_rows_ready, max_rows_set = sem("row_max_ready"), sem("max_rows_ready"), sem("max_rows_set")
        scored, exp_done, prob_slots_free, sums_done = (
            sem(n) for n in ("scored", "exp_done", "prob_slots_free", "sums_done"))
        q_ready, q_projected, q_copied, q_spread = sem("q_ready"), sem("q_projected"), sem("q_copied"), sem("q_spread")
        normed, transposed, transposed_copied = sem("normed"), sem("transposed"), sem("transposed_copied")
        flag_asked, flag_summed, flag_ready = sem("flag_asked"), sem("flag_summed"), sem("flag_ready")
        sums_copied, sums_turned = sem("sums_copied"), sem("sums_turned")
        weights_ready = sem("weights_ready")
        q2_projected, k2_projected, v2_projected, q2_copied, k2_copied, v2_copied = (
            sem(n) for n in ("q2_projected", "k2_projected", "v2_projected", "q2_copied", "k2_copied", "v2_copied"))
        self_scored, self_shifted, self_exp, probs_turned, self_attended = (
            sem(n) for n in ("self_scored", "self_shifted", "self_exp", "probs_turned", "self_attended"))
        even_copied, odd_copied = sem("even_copied"), sem("odd_copied")
        wv_ready, wv_turned, wv_copied, wo_done = sem("wv_ready"), sem("wv_turned"), sem("wv_copied"), sem("wo_done")
        peak_ready, peak_spread = sem("peak_ready"), sem("peak_spread")
        ffn_projected, gate_ready, sig_ready = sem("ffn_projected"), sem("gate_ready"), sem("sig_ready")
        up_scale_ready, up_shifted, up_clipped, up_unshifted, both_scales_ready, up_scaled = (
            sem(n) for n in ("up_scale_ready", "up_shifted", "up_clipped", "up_unshifted", "both_scales_ready", "up_scaled"))
        o_ready, o_turned, o0_copied, o1_copied, down_done, result_ready = (
            sem(n) for n in ("o_ready", "o_turned", "o0_copied", "o1_copied", "down_done", "result_ready"))
        dve_steps = sem("dve_steps")

        s_probs = middle[:, 0:H * Q].rearrange("p (h k) -> p h k", h=H)
        s_probs_t = middle[:, H * Q:2 * H * Q].rearrange("p (h q) -> p h q", h=H)
        w_blocks = w_raw.rearrange("p (n b) -> p n b", b=BLOCK)
        ffn_wt = w_raw[:, DC * F:].rearrange("p (w c o) -> p w c o", w=2, c=DC)
        down_wt = wqr[:, 0:FT * D].rearrange("p (t o) -> p t o", t=FT)
        q2_pad = late[:, 0:H * Q].rearrange("p (h q) -> p h q", h=H)
        k2_t = late[:, H * Q:H * Q + DC * Q].rearrange("p (m k) -> p m k", m=DC)
        v2_sb = late[:, 2304:2304 + H * VW].rearrange("p (h w) -> p h w", h=H)
        sums_sb = late[:, 2688:3200]
        up_q, gate_q = late[:, 0:F], late[:, F:2 * F]
        sig = late[:, 2 * F:3 * F]
        qr = v_in[0:SR, 0:PR * Q].rearrange("p (a q) -> p a q", a=PR)
        qh = v_in[0:SR, PR * Q:2 * PR * Q].rearrange("p (a q) -> p a q", a=PR)
        hidden = late[:, 3 * F:4 * F]
        hidden_t = middle[:, 0:F].rearrange("p (t q) -> p t q", t=FT)

        def scored_in(slot):
            return (1, slot + LAG) if slot < H - LAG else (0, slot - (H - LAG))

        block = enter(nc.Block())

        @block.sync
        def _(sp):
            sp.dma_start(x0[:], x_d).then_inc(x_in, 16)
            sp.dma_start(ctx_t, ctx_d[0]).then_inc(ctx_in, 16)
            sp.dma_start(eye[:], eye_d).then_inc(eye_in, 16)
            sp.dma_start(wqn[:], wqn_d).then_inc(wqn_in, 16)
            sp.dma_start(w_kv[:, 0:DC * D], wk_d.rearrange("p c n -> p (c n)")).then_inc(wkv_in, 16)
            sp.dma_start(w_kv[:, DC * D:], wv_d.rearrange("p c n -> p (c n)")).then_inc(wkv_in, 16)
            sp.dma_start(wqr[:, :], wqr_d).then_inc(wqr_in, 16)
            sp.dma_start(bqn[:], bqn_d).then_inc(bq_in, 16)
            sp.dma_start(bqr[0:SR, :], bqr_d).then_inc(bq_in, 16)
            sp.dma_start(head_mask[:], headmask_d).then_inc(masks_in, 16)
            sp.dma_start(pair_mask[0:SR, :], pairmask_d).then_inc(masks_in, 16)
            sp.dma_start(causal[:], causal_d).then_inc(masks_in, 16)
            sp.dma_start(bk[:], bk_d).then_inc(bk_in, 16)
            sp.dma_start(mask_all.rearrange("p (b k) -> p b k", b=NB), maskn_d.rearrange("b p k -> p b k")).then_inc(mask_all_in, 16)
            sp.dma_start(mask_w[:, 0, :], maskn_d[0]).then_inc(mask_in[0], 16)
            sp.wait_ge(ctx_split, 1)
            sp.dma_start(ctx_t, ctx_d[1]).then_inc(ctx_in, 16)
            sp.dma_start(mask_w[:, 1, :], maskn_d[1]).then_inc(mask_in[1], 16)
            sp.dma_start(bv[:], bv_d).then_inc(bv_in, 16)
            sp.dma_start(wqvk[:], wqvk_d).then_inc(attn_w_in, 16)
            sp.dma_start(wo[:], wo_d).then_inc(attn_w_in, 16)

            def load(s, par):
                sp.wait_ge(ctx_split, s)
                sp.dma_start(ctx_t, ctx_d[s]).then_inc(ctx_in, 16)
                sp.dma_start(mask_w[:, par, :], maskn_d[s]).then_inc(mask_in[par], 16)

            def store(s, par):
                for m in range(DC):
                    sp.wait_ge(hi_ready, s * DC + m + 1)
                    sp.dma_start(k_hi_d[s, m], k_hi[:, par, m, :].bitcast(f32)).then_inc(hi_stored[par][m], 16)
                    sp.wait_ge(lo_ready, s * DC + m + 1)
                    sp.dma_start(k_lo_d[s, m], k_lo[:, m, :].bitcast(f32)).then_inc(lo_stored[m], 16)
                sp.wait_ge(v_evacuated, s * NV + NV)
                sp.dma_start(v_d[s], v_new[:, par].rearrange("p t h w -> p (t h w)")).then_inc(v_stored[par], 16)

            with sp.Fori(1, NB // 2) as i:
                load(i * 2, 0)
                store(i * 2 - 2, 0)
                load(i * 2 + 1, 1)
                store(i * 2 - 1, 1)

            def load_keys(b, par):
                for m in range(DC):
                    for slot in range(SLOTS):
                        src = (k_lo_d if slot == 2 else k_hi_d)[b, m]
                        sp.dma_start(k_stack[slot * 32:slot * 32 + 32, par, m * PR // 2:(m + 1) * PR // 2, :].bitcast(f32),
                                     src.rearrange("(p r) k -> r p k", r=2 * HD)).then_inc(stack_in[par], 16)

            def load_values(b, par):
                sp.dma_start(v_in[:, par * T * H * VW:(par + 1) * T * H * VW], v_d[b]).then_inc(v_back[par], 16)

            for b in range(2):
                if b == 1:
                    store(NB - 2, 0)
                    store(NB - 1, 1)
                    sp.wait_ge(v_projected, NB * NV)
                for m in range(DC):
                    sp.wait_ge(hi_stored[b][m], 16)
                    sp.wait_ge(lo_stored[m], 16 * (b + 1))
                load_keys(b, b)
            sp.wait_ge(w_split, 1)
            sp.wait_ge(q_spread, 6)
            for b in range(2):
                sp.wait_ge(v_stored[b], 16)
                load_values(b, b)
            for m in range(DC):
                for par in range(2):
                    sp.wait_ge(hi_stored[par][m], 16 * NB // 2)
                sp.wait_ge(lo_stored[m], 16 * NB)
            for par in range(2):
                sp.wait_ge(v_stored[par], 16 * NB // 2)
            sp.wait_ge(lo_ready, NB * DC)
            sp.wait_ge(row_max_ready, NB + 1)
            sp.dma_start(w_raw[:, 0:DC * F], wup_d).then_inc(ffn_w_in, 16)
            sp.dma_start(w_raw[:, DC * F:2 * DC * F], wgate_d).then_inc(ffn_w_in, 16)
            sp.dma_start(w_raw[:, 2 * DC * F:], wdown_d).then_inc(ffn_w_in, 16)
            with sp.Fori(1, NB // 2) as i:
                for par in range(2):
                    b = i * 2 + par
                    sp.wait_ge(prob_slots_free, (b - 1) * UNITS + SLOTS_P)
                    load_keys(b, par)
                    load_values(b, par)
            sp.wait_ge(out_stored, 16)

        @block.gpsimd
        def _(pool):
            fills = ((zeros_b[:], 0.0),
                     (early[:, o2:], 1.0),
                     (ones_c[:], 1.0), (magic[:, 0:1], MAGIC), (magic[:, 1:2], -MAGIC),
                     (k_stack[SR:SR + 1, 0, 0:PR // 2, :].bitcast(f32), 1.0),
                     (run_late[:, :, :], LEAST),
                     (k_stack[SR:SR + 1, 0, PR // 2:, :].bitcast(f32), 1.0))
            for n, (fill, value) in enumerate(fills[:-2]):
                nc.gpsimd.memset(fill, value).then_inc(consts_set, 1)
                pool.wait_ge(consts_set, n + 1)

            def split_context(s, par):
                pool.wait_ge(ctx_hi_ready, s + 1)
                nc.gpsimd.tensor_tensor(ctx_lo[:, par].rearrange("p c k -> p (c k)"), ctx_t,
                                        ctx_hi[:, par].rearrange("p c k -> p (c k)").bitcast(f32),
                                        ALU.subtract).then_inc(ctx_split, 1)

            def split(s, par, first, last=False):
                def next_context():
                    split_context(s + 1, 1 - par)
                    pool.wait_ge(ctx_split, s + 2)

                if not last and not (first and par == 0):
                    pool.wait_ge(lo_ready, s * DC)
                    next_context()
                if not first:
                    pool.wait_ge(max_scored, (s - 1) * H)
                for m in range(DC):
                    if m or last:
                        pool.wait_ge(lo_ready, s * DC + m)
                    if first and par == 0 and m == 1:
                        next_context()
                    pool.wait_ge(k_evacuated, (s * DC + m + 1) * 2)
                    if not first:
                        pool.wait_ge(hi_stored[par][m], (s - par) * 8)
                    nc.gpsimd.tensor_tensor(k_hi[:, par, m, :], kf[:, m, :], ones_c[:, 0:1].to_broadcast([P, BK]),
                                            ALU.mult).then_inc(hi_ready, 1)
                    pool.wait_ge(hi_ready, s * DC + m + 1)
                    if not (first and par == 0):
                        pool.wait_ge(lo_stored[m], s * 16)
                    nc.gpsimd.tensor_tensor(k_lo[:, m, :], kf[:, m, :], k_hi[:, par, m, :].bitcast(f32),
                                            ALU.subtract).then_inc(lo_ready, 1)

            split_context(0, 0)
            pool.wait_ge(ctx_split, 1)
            for n, (fill, value) in enumerate(fills[-2:]):
                nc.gpsimd.memset(fill, value).then_inc(consts_set, 1)
                pool.wait_ge(consts_set, len(fills) - 1 + n)
            split(0, 0, True)
            split(1, 1, True)
            with pool.Fori(1, NB // 2 - 1) as i:
                split(i * 2, 0, False)
                split(i * 2 + 1, 1, False)
            split(NB - 2, 0, False)
            split(NB - 1, 1, False, last=True)
            pool.wait_ge(lo_ready, NB * DC)
            lo = slice(32, 64)
            for ab in range(2):
                only = pair_mask[:, ab:ab + 1].unsqueeze(2).to_broadcast([P, PR, Q])
                nc.gpsimd.tensor_tensor(q_stack[0:SR, :, ab, :], qr, only[0:SR], ALU.mult).then_inc(q_spread, 1)
                pool.wait_ge(q_spread, 3 * ab + 1)
                nc.gpsimd.tensor_tensor(qh[lo], qr[lo], only[lo], ALU.mult).then_inc(q_spread, 1)
                pool.wait_ge(q_spread, 3 * ab + 2)
                nc.gpsimd.tensor_tensor(q_stack[lo, :, ab, :], qh[lo], q_stack[lo, :, ab, :].bitcast(f32),
                                        ALU.subtract).then_inc(q_spread, 1)
                pool.wait_ge(q_spread, 3 * ab + 3)
            pool.wait_ge(v_projected, NB * NV)
            nc.gpsimd.memset(k_stack[SR:SR + 1, 1, :, :].bitcast(f32), 1.0).then_inc(consts_set, 1)
            pool.wait_ge(mask_cast, NB)
            for b in range(2):
                pool.dma_start(mask_w[:, b, :], maskt_d[b]).then_inc(mask_t_in[b], 16)
            with pool.Fori(1, NB // 2) as i:
                for par in range(2):
                    pool.wait_ge(mask_cast, i * 2 + par + NB - 1)
                    pool.dma_start(mask_w[:, par, :], maskt_d[i * 2 + par]).then_inc(mask_t_in[par], 16)

        @block.scalar
        def _(act):
            def high_context(s, par):
                act.wait_ge(ctx_in, s * 16 + 16)
                nc.scalar.copy(ctx_hi[:, par].rearrange("p c k -> p (c k)"), ctx_t).then_inc(ctx_hi_ready, 1)

            high_context(0, 0)
            act.wait_ge(bk_in, 16)
            act.wait_ge(consts_set, 5)

            def evacuate_keys(s, m, n, first):
                act.wait_ge(k_projected, (s * DC + m) * 2 + n + 1)
                if not first and n == 0:
                    act.wait_ge(lo_ready, (s - 1) * DC + m + 1)
                nc.scalar.activation(kf[:, m, n * HK:(n + 1) * HK], ps_k[:, 0:HK], ACT.Identity,
                                     bias=bk[:, m:m + 1]).then_inc(k_evacuated, 1)

            def evacuate_values(s, par, k):
                act.wait_ge(v_projected, s * NV + k + 1)
                tiles = V_TILES[k]
                nc.scalar.copy(v_new[:, par, tiles[0]:tiles[-1] + 1, :, 0:HD],
                               ps_v[:, 0:len(tiles) * D].rearrange("p (t h d) -> p t h d", t=len(tiles), h=H)
                               ).then_inc(v_evacuated, 1)

            def copy_scores(s, par, h):
                k = VIA_ACT.index(h)
                act.wait_ge(max_scored, s * H + h + 1)
                if not (isinstance(s, int) and s == 0 and k < 2):
                    act.wait_ge(run_taken, s * NA + k - 1)
                nc.scalar.copy(staged[:, (par * NA + k) % 2, :].rearrange("p (n k) -> p n k", n=2),
                               ps_a[:, 2 * BUFFER[par][h]:2 * BUFFER[par][h] + 2, 0:HK]).then_inc(max_copied, 1)

            def evacuate(s, par, first, last=False):
                def prepare():
                    act.wait_ge(mask_in[par], (s - par) * 8 + 16)
                    if not first:
                        act.wait_ge(max_scored, (s - 1) * H)
                    nc.scalar.copy(mask_b[:, par, :], mask_u[:, par, :]).then_inc(mask_cast, 1)
                    if not last:
                        if not (first and par == 0):
                            act.wait_ge(v_projected, s * NV)
                        high_context(s + 1, 1 - par)

                if not first:
                    prepare()
                    act.wait_ge(v_stored[par], (s - par) * 8)
                for slot, work in enumerate(PROJECTIONS):
                    if first and slot == PREPARE_SLOTS[par]:
                        prepare()
                    if work and work[0] == "v":
                        evacuate_values(s, par, work[1])
                    if work and work[0] == "k":
                        evacuate_keys(s, work[1], work[2], first and par == 0)
                    of_last, h = scored_in(slot)
                    if h in VIA_ACT and not (of_last and first and par == 0):
                        copy_scores(s - of_last, (1 - par) if of_last else par, h)

            evacuate(0, 0, True)
            evacuate(1, 1, True)
            with act.Fori(1, NB // 2 - 1) as i:
                evacuate(i * 2, 0, False)
                evacuate(i * 2 + 1, 1, False)
            evacuate(NB - 2, 0, False)
            evacuate(NB - 1, 1, False, last=True)
            for h in range(LAG, H):
                if h in VIA_ACT:
                    copy_scores(NB - 1, 1, h)

            act.wait_ge(max_rows_ready, 1)
            nc.scalar.mul(q_stack[SR:SR + 1, 0:PR // 2, :, :].rearrange("p a b q -> p (a b q)"),
                          ps_a[SR:SR + 1, 0:2, :].rearrange("p a q -> p (a q)"), 1.0).then_inc(max_rows_set, 1)

            for par in range(2):
                act.wait_ge(v_stored[par], 16 * NB // 2)
            with act.Fori(0, NB // 2) as i:
                for u in range(2 * UNITS):
                    n = i * 2 * UNITS + u
                    act.wait_ge(scored, n + 1)
                    act.wait_ge(prob_slots_free, n + 1)
                    width = len(GROUPS[u % UNITS]) * 2 * Q
                    nc.scalar.activation(probs[u % SLOTS_P][:, 0:width],
                                         ps_a[:, 3 * (u % 2):3 * (u % 2) + 3, :].rearrange("p a n -> p (a n)")[:, 0:width],
                                         ACT.Exp).then_inc(exp_done, 1)

            act.wait_ge(k2_projected, 1)
            nc.scalar.copy(k2_t.rearrange("p m k -> p (m k)"), ps_v[:, 0:D]).then_inc(k2_copied, 1)
            act.wait_ge(v2_projected, 1)
            nc.scalar.copy(v2_sb[:, :, 0:HD], ps_k[:, D:2 * D].rearrange("p (h d) -> p h d", h=H)).then_inc(v2_copied, 1)
            def copy_odd(g):
                act.wait_ge(probs_turned, g + 1)
                nc.scalar.copy(s_probs_t[:, 4 * g:4 * g + 4, :].rearrange("p h q -> p (h q)"),
                               turn_banks[g]).then_inc(odd_copied, 1)

            for g in range(4):
                act.wait_ge(self_shifted, g + 1)
                if g % 2 == 0:
                    for k in range(4):
                        h = 4 * g + k
                        last = nc.scalar.activation(s_probs[:, h, :], ps_a[:, g, k * Q:(k + 1) * Q], ACT.Exp,
                                                    bias=block_max[:, 1, h:h + 1], scale=1.0 / D ** 0.5)
                else:
                    last = nc.scalar.activation(s_probs[:, 4 * g:4 * g + 4, :], s_probs[:, 4 * g:4 * g + 4, :], ACT.Exp,
                                                scale=1.0 / D ** 0.5)
                last.then_inc(self_exp, 1)
                if g == 2:
                    copy_odd(1)
            copy_odd(3)
            nc.scalar.activation(stats[:, 23:24], magic[:, 0:1], ACT.Sigmoid)
            act.wait_ge(gate_ready, 1)
            nc.scalar.activation(sig, gate_q, ACT.Sigmoid, scale=65536.0).then_inc(sig_ready, 1)
            act.wait_ge(up_scale_ready, 1)
            nc.scalar.activation(up_q.rearrange("p (n f) -> p n f", n=2), ps_a[:, 0:2, 0:FH], ACT.Identity,
                                 bias=magic[:, 0:1], scale=small[:, 13:14]).then_inc(up_shifted, 1)
            act.wait_ge(up_clipped, 1)
            nc.scalar.activation(up_q, up_q, ACT.Identity, bias=magic[:, 1:2]).then_inc(up_unshifted, 1)
            act.wait_ge(up_unshifted, 1)
            act.wait_ge(both_scales_ready, 1)
            nc.scalar.activation(up_q, up_q, ACT.Copy, scale=small[:, 14:15]).then_inc(up_scaled, 1)
            act.wait_ge(o_turned, 1)
            nc.scalar.activation(hidden_t[:, 0:3, :].rearrange("p t q -> p (t q)"), turn_banks[0][:, 0:3 * Q],
                                 ACT.Identity, bias=magic[:, 1:2]).then_inc(o0_copied, 1)
            act.wait_ge(result_ready, 1)
            act.dma_start(out_d, x3[:]).then_inc(out_stored, 16)

        @block.vector
        def _(dve):
            steps = [0]

            def link(instruction):
                steps[0] += 1
                instruction.then_inc(dve_steps, 1)
                dve.wait_ge(dve_steps, steps[0])

            def layernorm(src):
                link(nc.vector.bn_stats(stats[:, 0:6], src))
                link(nc.vector.bn_aggr(stats[:, 8:10], stats[:, 0:6]))
                link(nc.vector.tensor_scalar(small[:, 0:1], stats[:, 9:10], 1e-5, None, ALU.add))
                nc.vector.tensor_scalar(small[:, 1:2], small[:, 0:1], -0.5, None, ALU.mult)
                link(nc.vector.tensor_scalar(small[:, 2:3].bitcast(i32), small[:, 0:1].bitcast(i32), -0.5, ROOT_GUESS,
                                             ALU.mult, ALU.add))
                for n in range(3):
                    y, better = small[:, 2 + n:3 + n], small[:, 3 + n:4 + n]
                    link(nc.vector.tensor_scalar(small[:, 6:7], y, y, small[:, 1:2], ALU.mult, ALU.mult))
                    link(nc.vector.tensor_scalar(better, small[:, 6:7], 1.5, y, ALU.add, ALU.mult))
                return nc.vector.tensor_scalar(xn[:], src, stats[:, 8:9], small[:, 5:6], ALU.subtract, ALU.mult)

            def copy_turned(nth, psum):
                dve.wait_ge(transposed, nth)
                nc.vector.tensor_copy(xt[:, :, :].rearrange("p c q -> p (c q)"), psum).then_inc(transposed_copied, 1)

            dve.wait_ge(x_in, 16)
            layernorm(x0[:]).then_inc(normed, 1)
            copy_turned(1, ps_a[:, 0, 0:D])
            dve.wait_ge(wkv_in, 32)
            link(nc.vector.tensor_copy(w_hi[:, :, :, :].rearrange("p w c n -> p (w c n)"), w_kv))
            nc.vector.tensor_tensor(w_lo[:, :, :, :].rearrange("p w c n -> p (w c n)"), w_kv,
                                    w_hi[:, :, :, :].rearrange("p w c n -> p (w c n)").bitcast(f32),
                                    ALU.subtract).then_inc(w_split, 1)
            dve.wait_ge(eye_in, 16)
            nc.vector.tensor_scalar(big_eye[:], eye[:], BIG, None, ALU.mult)
            nc.vector.tensor_copy(eye_b[:], eye[:])
            dve.wait_ge(bq_in, 32)
            dve.wait_ge(masks_in, 48)
            nc.vector.tensor_copy(causal_b[:], causal[:])
            dve.wait_ge(q_projected, 1)
            for m in range(DC):
                link(nc.vector.tensor_scalar(x3[:, m * Q:(m + 1) * Q], ps_a[:, 1, m * Q:(m + 1) * Q], bqn[:, m:m + 1],
                                             HD ** -0.5, ALU.add, ALU.mult))
            for m in range(DC):
                last = nc.vector.tensor_tensor(
                    q_pad[:, m * HT:(m + 1) * HT, :],
                    x3[:, m * Q:(m + 1) * Q].unsqueeze(1).to_broadcast([P, HT, Q]),
                    head_mask[:, :].unsqueeze(2).to_broadcast([P, HT, Q]), ALU.mult)
            last.then_inc(q_ready, 1)
            nc.vector.memset(row_max[:], LEAST)
            nc.vector.memset(run_early, LEAST)
            dve.wait_ge(q_projected, 2)
            link(nc.vector.tensor_scalar(bqr[0:SR, :], bqr[0:SR, :], HD ** -0.5, None, ALU.mult))
            nc.vector.scalar_tensor_tensor(qr, ps_a[0:SR, 2:4, :].rearrange("p a (b q) -> p (a b) q", q=Q), HD ** -0.5,
                                           bqr[0:SR, :].unsqueeze(2).to_broadcast([SR, PR, Q]), ALU.mult,
                                           ALU.add).then_inc(q_copied, 1)
            dve.wait_ge(mask_all_in, 16)
            nc.vector.tensor_reduce(flag_f[:], mask_all, AX.X, ALU.max).then_inc(flag_asked, 1)
            dve.wait_ge(flag_summed, 1)
            nc.vector.tensor_scalar(flag_i[0:1, 0:1], ps_a[0:1, 5, 0:1], 0.0, None, ALU.is_gt).then_inc(flag_ready, 1)
            dve.wait_ge(consts_set, 7)

            def running(h):
                k = VIA_ACT.index(h)
                return run_early[:, k, :] if k < 2 else run_late[:, k - 2, :]

            def maxima(s, par):
                taken = 0
                for h in range(H):
                    if h in VIA_ACT:
                        k = VIA_ACT.index(h)
                        dve.wait_ge(max_copied, s * NA + k + 1)
                        nc.vector.tensor_tensor(running(h), running(h), staged[:, (par * NA + k) % 2, :], ALU.max).then_inc(run_taken, 1)
                        continue
                    dve.wait_ge(max_scored, s * H + h + 1)
                    nc.vector.tensor_reduce(block_max[:, par, taken:taken + 1], ps_a[:, 2 * BUFFER[par][h]:2 * BUFFER[par][h] + 2, 0:HK],
                                            AX.XY, ALU.max).then_inc(max_taken, 1)
                    taken += 1
                dve.wait_ge(max_taken, s * ND + ND)
                nc.vector.tensor_tensor(row_max[:, 0:ND], row_max[:, 0:ND], block_max[:, par, 0:ND],
                                        ALU.max).then_inc(row_max_ready, 1)
                dve.wait_ge(row_max_ready, s + 1)
                dve.wait_ge(run_taken, s * NA + NA)

            with dve.Fori(0, NB // 2) as i:
                maxima(i * 2, 0)
                maxima(i * 2 + 1, 1)
            for tiles, at in ((run_early, ND), (run_late[:, :, :], ND + 2)):
                width = BK // 2
                while width >= BK // 8:
                    link(nc.vector.tensor_tensor(tiles[:, :, 0:width], tiles[:, :, 0:width], tiles[:, :, width:2 * width],
                                                 ALU.max))
                    width //= 2
                link(nc.vector.tensor_reduce(row_max[:, at:at + tiles.shape[1]], tiles[:, :, 0:2 * width], AX.X, ALU.max))

            nc.vector.tensor_scalar(neg_max[:], row_max[:], -1.0, None, ALU.mult).then_inc(row_max_ready, 1)
            dve.wait_ge(max_rows_ready, 2)
            nc.vector.tensor_scalar(q_stack[SR:SR + 1, PR // 2:PR, :, :].rearrange("p a b q -> p (a b q)"),
                                    ps_a[SR:SR + 1, 2:4, :].rearrange("p a q -> p (a q)"), 1.0, None,
                                    ALU.mult).then_inc(max_rows_set, 1)

            def cast_mask(par, nth_load, used):
                dve.wait_ge(mask_t_in[par], nth_load)
                dve.wait_ge(scored, used)
                nc.vector.tensor_copy(mask_b[:, par, :], mask_u[:, par, :]).then_inc(mask_cast, 1)

            for b in range(2):
                cast_mask(b, 16, 0)

            dve.wait_ge(ffn_w_in, 48)
            scale_b = w_scale[:, :].unsqueeze(2).to_broadcast([P, WN // BLOCK, BLOCK])
            rec_b = w_rec[:, :].unsqueeze(2).to_broadcast([P, WN // BLOCK, BLOCK])
            link(nc.vector.tensor_reduce(w_scale[:], w_blocks, AX.X, ALU.max, apply_absolute_value=True))
            link(nc.vector.tensor_scalar(w_scale[:], w_scale[:], 1.0 / 7.0, 1e-12, ALU.mult, ALU.max))
            link(nc.vector.reciprocal(w_rec[:], w_scale[:]))
            link(nc.vector.tensor_tensor(w_blocks, w_blocks, rec_b, ALU.mult))
            link(nc.vector.tensor_scalar(w_raw, w_raw, MAGIC, MAGIC, ALU.add, ALU.subtract))
            link(nc.vector.tensor_scalar(w_raw, w_raw, 7.0, -8.0, ALU.min, ALU.max))
            link(nc.vector.tensor_tensor(w_blocks, w_blocks, scale_b, ALU.mult))
            link(nc.vector.transpose(wqr[:, 0:FT * D], w_raw[:, 2 * DC * F:]))
            link(nc.vector.transpose(w_raw[:, 2 * DC * F:], w_raw[:, DC * F:2 * DC * F]))
            nc.vector.transpose(w_raw[:, DC * F:2 * DC * F], w_raw[:, 0:DC * F]).then_inc(weights_ready, 1)
            dve.wait_ge(bv_in, 16)
            link(nc.vector.tensor_tensor(x1[:], x0[:], bv[:], ALU.add))

            with dve.Fori(1, NB // 2) as i:
                for par in range(2):
                    cast_mask(par, i * 16 + 16, (i * 2 + par - 1) * UNITS)

            dve.wait_ge(sums_done, 1)
            nc.vector.tensor_copy(sums_sb, attended).then_inc(sums_copied, 1)
            dve.wait_ge(sums_turned, 1)
            turned = ps_x.rearrange("p (h r) -> p h r", r=32)
            link(nc.vector.reciprocal(stats[:, 0:H], turned[:, :, HD]))
            link(nc.vector.tensor_tensor(xn[:, :].rearrange("p (h d) -> p h d", h=H), turned[:, :, 0:HD],
                                         stats[:, 0:H].unsqueeze(2).to_broadcast([P, H, HD]), ALU.mult))
            link(nc.vector.tensor_tensor(x1[:], x1[:], xn[:], ALU.add))

            layernorm(x1[:]).then_inc(normed, 1)
            copy_turned(2, ps_k[:, 0:D])
            nc.vector.memset(v2_sb[:, :, HD:VW], 1.0)
            for m in range(DC):
                dve.wait_ge(q2_projected, m + 1)
                nc.vector.tensor_tensor(
                    q2_pad[:, m * HT:(m + 1) * HT, :],
                    ps_a[:, 4 + m, 0:Q].unsqueeze(1).to_broadcast([P, HT, Q]),
                    head_mask[:, :].unsqueeze(2).to_broadcast([P, HT, Q]), ALU.mult).then_inc(q2_copied, 1)

            def copy_even(g):
                dve.wait_ge(probs_turned, g + 1)
                nc.vector.tensor_copy(s_probs_t[:, 4 * g:4 * g + 4, :].rearrange("p h q -> p (h q)"),
                                      turn_banks[g]).then_inc(even_copied, 1)

            for g in range(4):
                dve.wait_ge(self_scored, g + 1)
                scores = ps_a[:, g, :].rearrange("p (h k) -> p h k", h=4)
                link(nc.vector.tensor_reduce(block_max[:, 0, 4 * g:4 * g + 4], scores, AX.X, ALU.max))
                if g % 2 == 0:
                    nc.vector.tensor_scalar(block_max[:, 1, 4 * g:4 * g + 4], block_max[:, 0, 4 * g:4 * g + 4],
                                            -1.0 / D ** 0.5, None, ALU.mult).then_inc(self_shifted, 1)
                    if g == 2:
                        copy_even(0)
                else:
                    nc.vector.tensor_tensor(s_probs[:, 4 * g:4 * g + 4, :], scores,
                                            block_max[:, 0, 4 * g:4 * g + 4].unsqueeze(2).to_broadcast([P, 4, Q]),
                                            ALU.subtract).then_inc(self_shifted, 1)
            copy_even(2)
            dve.wait_ge(self_attended, 1)
            summed = ps_x[:, 0:H * VW].rearrange("p (h w) -> p h w", h=H)
            link(nc.vector.reciprocal(stats[:, 0:H], summed[:, :, HD]))
            nc.vector.tensor_tensor(xn[:, :].rearrange("p (h d) -> p h d", h=H), summed[:, :, 0:HD],
                                    stats[:, 0:H].unsqueeze(2).to_broadcast([P, H, HD]), ALU.mult).then_inc(wv_ready, 1)
            dve.wait_ge(wv_turned, 1)
            nc.vector.tensor_copy(xt[:, :, :].rearrange("p c q -> p (c q)"), ps_k[:, 0:D]).then_inc(wv_copied, 1)
            dve.wait_ge(wo_done, 1)
            link(nc.vector.tensor_tensor(x2[:], ps_x[:, 0:D], x1[:], ALU.add))

            def ask_peak(views):
                for n, view in enumerate(views):
                    last = nc.vector.tensor_reduce(peak[:, n:n + 1], view, AX.X, ALU.max, apply_absolute_value=True)
                last.then_inc(peak_ready, 1)

            def scales(nth, count, at):
                dve.wait_ge(peak_spread, nth)
                link(nc.vector.tensor_reduce(small[:, at:at + 1], ps_x[:, 0:count * P], AX.X, ALU.max))
                link(nc.vector.tensor_scalar(small[:, at:at + 1], small[:, at:at + 1], 1.0 / 32767.0, 1e-12,
                                             ALU.mult, ALU.max))
                return nc.vector.reciprocal(small[:, at + 1:at + 2], small[:, at:at + 1])

            def round_up_to_magic(dst, src, at):
                link(nc.vector.tensor_scalar(dst, src, small[:, at + 1:at + 2], MAGIC, ALU.mult, ALU.add))
                return nc.vector.tensor_scalar(dst, dst, MAGIC + 32767.0, MAGIC - 32768.0, ALU.min, ALU.max)

            link(layernorm(x2[:]))
            ask_peak([xn[:]])
            link(scales(1, 1, 8))
            round_up_to_magic(xn[:], xn[:], 8).then_inc(normed, 1)
            dve.wait_ge(transposed, 3)
            nc.vector.tensor_scalar(xt[:, :, :].rearrange("p c q -> p (c q)"), ps_k[:, 0:D], MAGIC, small[:, 8:9],
                                    ALU.subtract, ALU.mult).then_inc(transposed_copied, 1)
            up_ps, gate_ps = ps_a[:, 0:2, 0:FH], ps_a[:, 2:4, 0:FH]
            for n in range(2):
                dve.wait_ge(ffn_projected, n + 1)
                last = nc.vector.tensor_reduce(peak[:, n:n + 1], gate_ps[:, n, :], AX.X, ALU.max, apply_absolute_value=True)
            last.then_inc(peak_ready, 1)
            link(scales(2, 2, 8))
            link(nc.vector.tensor_scalar(small[:, 10:11], small[:, 8:9], 1.0 / 65536.0, None, ALU.mult))
            link(round_up_to_magic(gate_q.rearrange("p (n f) -> p n f", n=2), gate_ps, 8))
            nc.vector.tensor_scalar(gate_q, gate_q, MAGIC, small[:, 10:11], ALU.subtract, ALU.mult).then_inc(gate_ready, 1)
            dve.wait_ge(ffn_projected, 4)
            ask_peak([up_ps[:, n, :] for n in range(2)])
            scales(3, 2, 12).then_inc(up_scale_ready, 1)
            dve.wait_ge(sig_ready, 1)
            link(nc.vector.tensor_scalar(sig, sig, 65536.0, MAGIC, ALU.mult, ALU.add))
            link(nc.vector.tensor_scalar(sig, sig, MAGIC + 65535.0, MAGIC, ALU.min, ALU.subtract))
            link(nc.vector.scalar_tensor_tensor(hidden, sig, 0.0, gate_q, ALU.max, ALU.mult))
            ask_peak([hidden])
            dve.wait_ge(up_shifted, 1)
            nc.vector.tensor_scalar(up_q, up_q, MAGIC + 32767.0, MAGIC - 32768.0, ALU.min, ALU.max).then_inc(up_clipped, 1)
            link(scales(4, 1, 8))
            nc.vector.tensor_scalar(small[:, 14:15], small[:, 8:9], small[:, 12:13], None, ALU.mult).then_inc(both_scales_ready, 1)
            link(round_up_to_magic(hidden, hidden, 8))
            dve.wait_ge(up_scaled, 1)
            link(nc.vector.scalar_tensor_tensor(hidden, hidden, MAGIC, up_q, ALU.subtract, ALU.mult))
            ask_peak([hidden])
            link(scales(5, 1, 8))
            for n in range(2):
                half = hidden[:, n * FH:(n + 1) * FH]
                round_up_to_magic(half, half, 8).then_inc(o_ready, 1)
            dve.wait_ge(o_turned, 2)
            nc.vector.tensor_scalar(hidden_t[:, 3:6, :].rearrange("p t q -> p (t q)"), turn_banks[1][:, 0:3 * Q],
                                    MAGIC, None, ALU.subtract).then_inc(o1_copied, 1)
            dve.wait_ge(down_done, 1)
            nc.vector.scalar_tensor_tensor(x3[:], ps_k[:, 0:D], small[:, 8:9], x2[:], ALU.mult, ALU.add).then_inc(result_ready, 1)

        @block.tensor
        def _(pe):
            part_pairs = ((w_hi, ctx_hi), (w_hi, ctx_lo), (w_lo, ctx_hi))
            terms = [(w, part, c) for w, part in part_pairs for c in range(DC)]

            def project_keys(s, par, m, n):
                if not (isinstance(s, int) and s == 0 and m == 0 and n == 0):
                    pe.wait_ge(k_evacuated, (s * DC + m) * 2 + n)
                for k, (w, part, c) in enumerate(terms):
                    last = nc.tensor.matmul(ps_k[:, 0:HK], w[:, 0, c, m * P:(m + 1) * P],
                                            part[:, par, c, n * HK:(n + 1) * HK], start=(k == 0), stop=(k == len(terms) - 1))
                last.then_inc(k_projected, 1)

            def project_values(s, par, k):
                if not (isinstance(s, int) and s == 0 and k == 0):
                    pe.wait_ge(v_evacuated, s * NV + k)
                for n, t in enumerate(V_TILES[k]):
                    for j, (w, part, c) in enumerate(terms):
                        last = nc.tensor.matmul(ps_v[:, n * D:(n + 1) * D], part[:, par, c, t * P:(t + 1) * P],
                                                w[:, 1, c, :], start=(j == 0), stop=(j == len(terms) - 1))
                last.then_inc(v_projected, 1)

            def project(s, par, slot):
                work = PROJECTIONS[slot]
                if work is None:
                    return
                if work[0] == "k":
                    project_keys(s, par, *work[1:])
                else:
                    project_values(s, par, work[1])

            def score_for_max(s, par, h, masked):
                m = h // HT
                if h % HT == 0:
                    pe.wait_ge(hi_ready, s * DC + m + 1)
                if h == 0 and masked:
                    pe.wait_ge(mask_cast, s + 1)
                pair = BUFFER[par][h]
                earlier = [a for a in range(h) if BUFFER[par][a] == pair]
                before = earlier[-1] if earlier else max(a for a in range(H) if BUFFER[1 - par][a] == pair)
                back = 0 if earlier else 1
                if not (isinstance(s, int) and s == 0 and back):
                    if before in VIA_ACT:
                        pe.wait_ge(max_copied, (s - back) * NA + VIA_ACT.index(before) + 1)
                    else:
                        rank = before - sum(a < before for a in VIA_ACT)
                        pe.wait_ge(max_taken, (s - back) * ND + rank + 1)
                for n in range(2):
                    out = ps_a[:, 2 * pair + n, 0:HK]
                    last = nc.tensor.matmul(out, q_pad[:, h, :], k_hi[:, par, m, n * HK:(n + 1) * HK],
                                            start=True, stop=not masked)
                    if masked:
                        last = nc.tensor.matmul(out, big_eye[:], mask_b[:, par, n * HK:(n + 1) * HK], start=False, stop=True)
                last.then_inc(max_scored, 1)

            def keep_clock(bank, count):
                for _ in range(count):
                    nc.tensor.matmul(bank, zeros_b[:, 0:P], zeros_b[:], start=True, stop=True)

            pe.wait_ge(consts_set, 1)
            keep_clock(ps_v[:, :], WARM_FIRST)
            pe.wait_ge(normed, 1)
            pe.wait_ge(eye_in, 16)
            for c in range(DC):
                last = nc.tensor.transpose(ps_a[:, 0, c * Q:(c + 1) * Q], xn[:, c * P:(c + 1) * P], eye[:])
            last.then_inc(transposed, 1)
            pe.wait_ge(transposed_copied, 1)
            pe.wait_ge(wqn_in, 16)
            for m in range(DC):
                for c in range(DC):
                    last = nc.tensor.matmul(ps_a[:, 1, m * Q:(m + 1) * Q], wqn[:, c, m * P:(m + 1) * P], xt[:, c, :],
                                            start=(c == 0), stop=(c == DC - 1))
            last.then_inc(q_projected, 1)
            pe.wait_ge(wqr_in, 16)
            wqr_v = wqr[:, :].rearrange("p (c a r) -> p c a r", c=DC, a=PR)
            for a in range(PR):
                for c in range(DC):
                    last = nc.tensor.matmul(ps_a[0:SR, 2 + a // 4, (a % 4) * Q:(a % 4 + 1) * Q], wqr_v[:, c, a, :], xt[:, c, :],
                                            start=(c == 0), stop=(c == DC - 1))
            last.then_inc(q_projected, 1)
            pe.wait_ge(w_split, 1)
            pe.wait_ge(ctx_split, 1)
            for slot in range(H - LAG):
                project(0, 0, slot)
            pe.wait_ge(flag_asked, 1)
            nc.tensor.matmul(ps_a[0:1, 5, 0:1], flag_f[:], ones_c[:], start=True, stop=True).then_inc(flag_summed, 1)
            pe.wait_ge(flag_ready, 1)
            masked_flag = pe.value_load(flag_i[0:1, 0:1], min_val=0, max_val=1)

            def attend(masked):
                pe.wait_ge(q_ready, 1)
                pe.wait_ge(q_copied, 1)

                def slots(s, par, which):
                    for slot in which:
                        project(s, par, slot)
                        of_last, h = scored_in(slot)
                        score_for_max(s - of_last, (1 - par) if of_last else par, h, masked)

                def step(s, par):
                    pe.wait_ge(ctx_split, s + 1)
                    slots(s, par, range(H))

                slots(0, 0, range(H - LAG, H))
                step(1, 1)
                with pe.Fori(1, NB // 2) as i:
                    step(i * 2, 0)
                    step(i * 2 + 1, 1)
                for h in range(LAG, H):
                    score_for_max(NB - 1, 1, h, masked)

                pe.wait_ge(row_max_ready, NB + 1)
                columns = [h for h in range(H) if h not in VIA_ACT] + list(VIA_ACT)
                for h in range(H):
                    last = nc.tensor.matmul(ps_a[SR:SR + 1, h // 4, (h % 4) * Q:(h % 4 + 1) * Q], neg_max[:, columns.index(h):columns.index(h) + 1], eye_b[:],
                                            start=True, stop=True)
                    if h % HT == HT - 1:
                        last.then_inc(max_rows_ready, 1)

                pe.wait_ge(k_evacuated, NB * DC * 2)
                nc.tensor.matmul(attended, zeros_b[:, 0:P], zeros_b[:], start=True, stop=True,
                                 skip_group_check=True).then_inc(prob_slots_free, SLOTS_P)
                pe.wait_ge(max_rows_set, 2)
                pe.wait_ge(q_spread, 6)
                pe.wait_ge(consts_set, 8)

                def score(b_par, u):
                    for k, g in enumerate(GROUPS[u]):
                        t, a = divmod(g, PR)
                        bank = 3 * (u % 2) + k // 2
                        last = nc.tensor.matmul(ps_a[:, bank, (k % 2) * 2 * Q:(k % 2 + 1) * 2 * Q],
                                                k_stack[0:SR + 1, b_par, a, t * P:(t + 1) * P],
                                                q_stack[0:SR + 1, a, :, :].rearrange("p b q -> p (b q)"),
                                                start=(k % 2 == 0), stop=(k % 2 == 1) and not masked, skip_group_check=True)
                        if masked and k % 2 == 1:
                            last = nc.tensor.matmul(ps_a[:, bank, :], big_eye[:],
                                                    mask_b[:, b_par, t * P:(t + 1) * P].unsqueeze(1).to_broadcast([P, 4, Q]),
                                                    start=False, stop=True, skip_group_check=True)
                    last.then_inc(scored, 1)

                def add_up(b_par, u, slot):
                    for k in range(2 * len(GROUPS[u])):
                        t, h = divmod(2 * GROUPS[u][0] + k, H)
                        j, c = h % 4, h // 4
                        last = nc.tensor.matmul(attended[32 * j:32 * j + VW, c * Q:(c + 1) * Q], v_ring[:, b_par, t, h, :],
                                                probs[slot][:, k * Q:(k + 1) * Q], start=False, stop=False,
                                                skip_group_check=True)
                    last.then_inc(prob_slots_free, 1)

                def arrive(b, par):
                    pe.wait_ge(stack_in[par], (b - par) * 48 + 96)
                    if masked:
                        pe.wait_ge(mask_cast, b + NB + 1)

                def two_blocks(i, final):
                    for u in range(2 * UNITS):
                        n = i * (2 * UNITS) + u
                        pe.wait_ge(exp_done, n + 1)
                        if not (final and u >= 2 * UNITS - 2):
                            nxt = (u + 2) % (2 * UNITS)
                            if nxt == 0:
                                arrive(i * 2 + 2, 0)
                            if nxt == UNITS:
                                pe.wait_ge(consts_set, 9)
                                arrive(i * 2 + 1, 1)
                            score(nxt // UNITS, nxt % UNITS)
                        if u % UNITS == 0:
                            pe.wait_ge(v_back[u // UNITS], i * 16 + 16)
                        add_up(u // UNITS, u % UNITS, u % SLOTS_P)

                arrive(0, 0)
                score(0, 0)
                score(0, 1)
                with pe.Fori(0, NB // 2 - 1) as i:
                    two_blocks(i, False)
                two_blocks(NB // 2 - 1, True)

            for masked in (False, True):
                with pe.If(masked_flag == int(masked)):
                    attend(masked)

            nc.tensor.matmul(ps_v[0:1, 0:1], zeros_b[:, 0:1], zeros_b[:, 0:1], start=True, stop=True).then_inc(sums_done, 1)
            pe.wait_ge(sums_copied, 1)
            for c in range(4):
                last = nc.tensor.transpose(ps_x[:, c * P:(c + 1) * P], sums_sb[:, c * P:(c + 1) * P], eye[:])
            last.then_inc(sums_turned, 1)

            def turn_rows(nth):
                pe.wait_ge(normed, nth)
                for c in range(DC):
                    last = nc.tensor.transpose(ps_k[:, c * Q:(c + 1) * Q], xn[:, c * P:(c + 1) * P], eye[:])
                last.then_inc(transposed, 1)
                pe.wait_ge(transposed_copied, nth)

            keep_clock(ps_v[:, :], WARM[0])
            turn_rows(2)
            pe.wait_ge(attn_w_in, 32)

            def project_rows(out, at):
                for c in range(DC):
                    last = nc.tensor.matmul(out, wqvk[:, c, at:at + P], xt[:, c, :], start=(c == 0), stop=(c == DC - 1))
                return last

            project_rows(ps_a[:, 4, 0:Q], 0).then_inc(q2_projected, 1)
            project_rows(ps_v[:, 0:Q], 2 * D)
            project_rows(ps_v[:, Q:2 * Q], 2 * D + P).then_inc(k2_projected, 1)
            project_rows(ps_a[:, 5, 0:Q], P).then_inc(q2_projected, 1)
            for c in range(DC):
                last = nc.tensor.matmul(ps_k[:, D:2 * D], xt[:, c, :], wqvk[:, c, D:2 * D], start=(c == 0), stop=(c == DC - 1))
            last.then_inc(v2_projected, 1)
            pe.wait_ge(k2_copied, 1)
            for g in range(4):
                if g % 2 == 0:
                    pe.wait_ge(q2_copied, g // 2 + 1)
                for k in range(4):
                    h = 4 * g + k
                    nc.tensor.matmul(ps_a[:, g, k * Q:(k + 1) * Q], q2_pad[:, h, :], k2_t[:, h // HT, :], start=(k == 0),
                                     stop=False, skip_group_check=True)
                nc.tensor.matmul(ps_a[:, g, :], big_eye[:], causal_b[:, :].unsqueeze(1).to_broadcast([P, 4, Q]),
                                 start=False, stop=True, skip_group_check=True).then_inc(self_scored, 1)
            pe.wait_ge(v2_copied, 1)

            def turn_probs(g):
                pe.wait_ge(self_exp, g + 1)
                for k in range(4):
                    last = nc.tensor.transpose(turn_banks[g][:, k * P:(k + 1) * P], s_probs[:, 4 * g + k, :], eye[:])
                last.then_inc(probs_turned, 1)

            def attend_self(g):
                pe.wait_ge(odd_copied if g % 2 else even_copied, g // 2 + 1)
                for k in range(4):
                    h = 4 * g + k
                    last = nc.tensor.matmul(ps_x[:, h * VW:(h + 1) * VW], s_probs_t[:, h, :], v2_sb[:, h, :],
                                            start=True, stop=True, skip_group_check=True)
                return last

            for g in range(3):
                turn_probs(g)
            attend_self(0)
            attend_self(1)
            turn_probs(3)
            attend_self(2)
            attend_self(3).then_inc(self_attended, 1)
            keep_clock(ps_v[:, :], WARM[7])
            pe.wait_ge(wv_ready, 1)
            for c in range(DC):
                last = nc.tensor.transpose(ps_k[:, c * Q:(c + 1) * Q], xn[:, c * P:(c + 1) * P], eye[:])
            last.then_inc(wv_turned, 1)
            pe.wait_ge(wv_copied, 1)
            for c in range(DC):
                last = nc.tensor.matmul(ps_x[:, 0:D], xt[:, c, :], wo[:, c, :], start=(c == 0), stop=(c == DC - 1))
            last.then_inc(wo_done, 1)

            def spread_peaks(nth, count):
                pe.wait_ge(peak_ready, nth)
                for n in range(count):
                    last = nc.tensor.matmul(ps_x[:, n * P:(n + 1) * P], peak[:, n:n + 1].to_broadcast([P, P]), eye[:],
                                            start=True, stop=True)
                last.then_inc(peak_spread, 1)

            keep_clock(ps_v[:, :], WARM[1])
            spread_peaks(1, 1)
            keep_clock(ps_v[:, :], WARM[2])
            turn_rows(3)
            pe.wait_ge(weights_ready, 1)
            for w in (1, 0):
                for n in range(2):
                    for c in range(DC):
                        last = nc.tensor.matmul(ps_a[:, 2 * w + n, 0:FH], xt[:, c, :], ffn_wt[:, w, c, n * FH:(n + 1) * FH],
                                                start=(c == 0), stop=(c == DC - 1))
                        if (w, n, c) == (0, 0, 0):
                            spread_peaks(2, 2)
                    last.then_inc(ffn_projected, 1)
            keep_clock(ps_v[:, :], WARM[3])
            spread_peaks(3, 2)
            keep_clock(ps_v[:, :], WARM[4])
            spread_peaks(4, 1)
            keep_clock(ps_v[:, :], WARM[5])
            spread_peaks(5, 1)
            keep_clock(ps_v[:, :], WARM[6])
            for t in range(FT):
                if t % 3 == 0:
                    pe.wait_ge(o_ready, t // 3 + 1)
                last = nc.tensor.transpose(turn_banks[t // 3][:, (t % 3) * Q:(t % 3 + 1) * Q], hidden[:, t * P:(t + 1) * P], eye[:])
                if t % 3 == 2:
                    last.then_inc(o_turned, 1)
            for t in range(FT):
                if t % 3 == 0:
                    pe.wait_ge(o1_copied if t else o0_copied, 1)
                last = nc.tensor.matmul(ps_k[:, 0:D], hidden_t[:, t, :], down_wt[:, t, :], start=(t == 0), stop=(t == FT - 1))
            last.then_inc(down_done, 1)


def kernel(x, ctx_1024, mask_BxSxS2_bf0, L0_xattn_Wq, L0_xattn_bq, L0_xattn_Wk, L0_xattn_bk, L0_xattn_Wv, L0_xattn_bv,
           L0_attn_Wqvk, L0_attn_Wo, L0_ffn_w_gate, L0_ffn_w_up, L0_ffn_w_down):
    import numpy as np
    import concourse.bacc as bacc
    from concourse.bass_utils import run_bass_kernel_spmd

    def chunks(w):
        return np.ascontiguousarray(np.asarray(w).reshape(-1, P, np.asarray(w).shape[1]).transpose(1, 0, 2))

    def squares(w):
        n_out, n_in = np.asarray(w).shape
        w = np.asarray(w).reshape(n_out // 32, 32, n_in // P, P // 32, 32)
        return w.transpose(3, 1, 2, 0, 4).reshape(P, n_in // P * n_out)

    def words(a):
        return np.ascontiguousarray(a).view(np.int32)

    mask = np.asarray(mask_BxSxS2_bf0)[0].view(np.uint8)
    wq_t = chunks(np.asarray(L0_xattn_Wq).T)
    rows = np.arange(P)
    arrays = {
        "x": np.asarray(x)[0],
        "ctx": np.asarray(ctx_1024)[0].T.reshape(DC, P, NB, BK).transpose(2, 1, 0, 3),
        "maskn": words(mask.reshape(Q, NB, BK).transpose(1, 0, 2)),
        "maskt": words(mask.T.reshape(NB, T, P, Q).transpose(0, 2, 1, 3).reshape(NB, P, T * Q)),
        "wqn": wq_t,
        "wqr": np.broadcast_to(wq_t.reshape(P, DC, PR, 1, 2 * HD), (P, DC, PR, SLOTS, 2 * HD)).reshape(P, DC * PR * SR),
        "bqn": np.asarray(L0_xattn_bq).reshape(DC, P).T,
        "bqr": np.broadcast_to(np.asarray(L0_xattn_bq).reshape(1, PR, 2 * HD), (SLOTS, PR, 2 * HD)).transpose(0, 2, 1).reshape(SR, PR),
        "wk": chunks(np.asarray(L0_xattn_Wk).T),
        "bk": np.asarray(L0_xattn_bk).reshape(DC, P).T,
        "wv": chunks(np.asarray(L0_xattn_Wv).T),
        "bv": np.broadcast_to(np.asarray(L0_xattn_bv)[None, :], (P, D)),
        "wqvk": chunks(L0_attn_Wqvk),
        "wo": chunks(L0_attn_Wo),
        "wgate": squares(L0_ffn_w_gate),
        "wup": squares(L0_ffn_w_up),
        "wdown": squares(L0_ffn_w_down),
        "eye": np.eye(P, dtype=np.float32),
        "headmask": (rows[:, None] // HD == np.arange(HT)[None, :]).astype(np.float32),
        "pairmask": (rows[:SR, None] % 32 // HD == np.arange(2)[None, :]).astype(np.float32),
        "causal": (rows[None, :] > rows[:, None]).astype(np.float32),
    }
    nc = bacc.Bacc("TRN2", target_bir_lowering=False, num_devices=1)
    inputs, args = {}, []
    for name, a in arrays.items():
        a = np.ascontiguousarray(a)
        inputs[f"in_{name}"] = a
        args.append(nc.dram_tensor(f"in_{name}", a.shape, mybir.dt.from_np(a.dtype), kind="ExternalInput").ap())
    out = nc.dram_tensor("out", (Q, D), mybir.dt.float32, kind="ExternalOutput").ap()
    perceiver_layer(nc, *args, out)
    r = run_bass_kernel_spmd(nc, [inputs], core_ids=[0])
    return r.results[0]["out"].reshape(1, Q, D)
```
